# Optimizing a Trainium2 kernel written in Bass

```python
import numpy as np
import jax
import jax.numpy as jnp

def _softmax(x, axis=-1):
    return jax.nn.softmax(x, axis=axis)

def _gelu(x):
    return jax.nn.gelu(x, approximate=True)

def _silu(x):
    return jax.nn.silu(x)

def _sigmoid(x):
    return jax.nn.sigmoid(x)

def _layernorm(x, axis=-1, eps=1e-05):
    m = jnp.mean(x, axis=axis, keepdims=True)
    v = jnp.var(x, axis=axis, keepdims=True)
    return (x - m) / jnp.sqrt(v + eps)

def _scatter_add(tgt, idx, src, axis=0):
    return tgt.at[idx].add(src)

def _segment_sum(src, seg, n):
    return jax.ops.segment_sum(src, seg, n)
kernel_name = 'mk_pixart_seq_d1_seqx_r8_99ff40'

def setup_inputs(seed: int=0):
    np.random.seed(seed)
    _w = jnp.asarray

    def _rec_inputs():
        import jax
        import jax.numpy as jnp
        _rk = jax.random.key(seed)
        x = -0.0005207 + 1.001 * jax.random.normal(jax.random.fold_in(_rk, 1), (8, 256, 128), jnp.float32)
        _lenS = 256 - jax.random.randint(jax.random.fold_in(_rk, 7), (8,), 0, max(1, 256 // 4) + 1, jnp.int32)
        _lenS2 = 1601 - jax.random.randint(jax.random.fold_in(_rk, 8), (8,), 0, max(1, 1601 // 4) + 1, jnp.int32)
        cond_1024 = 0.000887014 + 1.03683 * jax.random.normal(jax.random.fold_in(_rk, 11), (8, 128), jnp.float32)
        _ctx_768P = jax.random.normal(jax.random.fold_in(_rk, 12), (8, 16, 96), jnp.float32)
        _ctx_768c = jax.random.dirichlet(jax.random.fold_in(_rk, 512), 0.3 * jnp.ones((16,), jnp.float32), (8, 1601))
        _ctx_768t = jnp.einsum('bsk,bkd->bsd', _ctx_768c, _ctx_768P)
        _ctx_768t = _ctx_768t * jax.lax.rsqrt(jnp.mean(jnp.square(_ctx_768t)) + 1e-12) * 0.953939
        ctx_768 = 0.000599585 + 1.00006 * (_ctx_768t + 0.3 * jax.random.normal(jax.random.fold_in(_rk, 612), (8, 1601, 96), jnp.float32))
        return (x, cond_1024, ctx_768)
    x, cond_1024, ctx_768 = _rec_inputs()

    def _L0_xcond_setup():
        import jax, jax.numpy as jnp
        import numpy as np
        B, N, M = (2, 128, 64)
        D, H, DH = (128, 16, 64)
        MID = H * DH
        DC = 96
        MULT = 4
        EPS = 1e-05

        def _ln(x, w, b):
            mu = jnp.mean(x, -1, keepdims=True)
            var = jnp.mean((x - mu) ** 2, -1, keepdims=True)
            return (x - mu) * jax.lax.rsqrt(var + EPS) * w + b

        def _sincos(n, d):
            inv = 1.0 / 10000.0 ** (jnp.arange(0, d, 2, dtype=jnp.float32) / d)
            ang = jnp.arange(n, dtype=jnp.float32)[:, None] * inv[None, :]
            return (jnp.sin(ang), jnp.cos(ang))

        def _rope(x, sin, cos):
            s = sin[None, None]
            c = cos[None, None]
            xe = x[..., ::2]
            xo = x[..., 1::2]
            re = xe * c - xo * s
            ro = xe * s + xo * c
            return jnp.stack((re, ro), axis=-1).reshape(x.shape)

        def _heads(t):
            b, n, _ = t.shape
            return t.reshape(b, n, H, DH).transpose(0, 2, 1, 3)

        def _attn(xq, ctx, wq, wkv, wo, bo):
            q = _heads(xq @ wq)
            k, v = jnp.split(ctx @ wkv, 2, axis=-1)
            k = _heads(k)
            v = _heads(v)
            sq, cq = _sincos(q.shape[2], DH)
            sk, ck = _sincos(k.shape[2], DH)
            q = _rope(q, sq, cq)
            k = _rope(k, sk, ck)
            sim = jnp.einsum('bhnd,bhmd->bhnm', q, k) * DH ** (-0.5)
            a = jax.nn.softmax(sim, axis=-1)
            o = jnp.einsum('bhnm,bhmd->bhnd', a, v)
            o = o.transpose(0, 2, 1, 3).reshape(xq.shape[0], xq.shape[1], MID)
            return o @ wo + bo

        def _adaln(x, c, lw, lb, gw, gb, bw, bb):
            g = (c @ gw + gb)[:, None, :]
            bt = (c @ bw + bb)[:, None, :]
            return _ln(x, lw, lb) * (1.0 + g) + bt
        ks = jax.random.split(jax.random.key(seed), 24)
        s = 0.02
        inp = {'x': jax.random.normal(ks[0], (B, N, D), jnp.float32), 'cond': jax.random.normal(ks[1], (B, D), jnp.float32), 'context': jax.random.normal(ks[2], (B, M, DC), jnp.float32), 'ln1_w': jnp.ones((D,), jnp.float32), 'ln1_b': jnp.zeros((D,), jnp.float32), 'g1_w': jax.random.normal(ks[3], (D, D), jnp.float32) * s, 'g1_b': jnp.zeros((D,), jnp.float32), 'b1_w': jax.random.normal(ks[4], (D, D), jnp.float32) * s, 'b1_b': jnp.zeros((D,), jnp.float32), 'ln2_w': jnp.ones((D,), jnp.float32), 'ln2_b': jnp.zeros((D,), jnp.float32), 'g2_w': jax.random.normal(ks[5], (D, D), jnp.float32) * s, 'g2_b': jnp.zeros((D,), jnp.float32), 'b2_w': jax.random.normal(ks[6], (D, D), jnp.float32) * s, 'b2_b': jnp.zeros((D,), jnp.float32), 'sa_wq': jax.random.normal(ks[7], (D, MID), jnp.float32) * s, 'sa_wkv': jax.random.normal(ks[8], (D, 2 * MID), jnp.float32) * s, 'sa_wo': jax.random.normal(ks[9], (MID, D), jnp.float32) * s, 'sa_bo': jnp.zeros((D,), jnp.float32), 'ca_lnc_w': jnp.ones((DC,), jnp.float32), 'ca_lnc_b': jnp.zeros((DC,), jnp.float32), 'ca_wq': jax.random.normal(ks[10], (D, MID), jnp.float32) * s, 'ca_wkv': jax.random.normal(ks[11], (DC, 2 * MID), jnp.float32) * s, 'ca_wo': jax.random.normal(ks[12], (MID, D), jnp.float32) * s, 'ca_bo': jnp.zeros((D,), jnp.float32), 'ff_w1': jax.random.normal(ks[13], (D, MULT * D), jnp.float32) * s, 'ff_b1': jnp.zeros((MULT * D,), jnp.float32), 'ff_w2': jax.random.normal(ks[14], (MULT * D, D), jnp.float32) * s, 'ff_b2': jnp.zeros((D,), jnp.float32)}
        return inp
    _L0_xcond_all = _L0_xcond_setup()
    _L0_xcond_in = {k: v for k, v in _L0_xcond_all.items() if k in ('ln1_w', 'ln1_b', 'g1_w', 'g1_b', 'b1_w', 'b1_b', 'ln2_w', 'ln2_b', 'g2_w', 'g2_b', 'b2_w', 'b2_b', 'sa_wq', 'sa_wkv', 'sa_wo', 'sa_bo', 'ca_lnc_w', 'ca_lnc_b', 'ca_wq', 'ca_wkv', 'ca_wo', 'ca_bo', 'ff_w1', 'ff_b1', 'ff_w2', 'ff_b2')}
    del _L0_xcond_all
    return {'x': x, 'cond_1024': cond_1024, 'ctx_768': ctx_768, 'L0_xcond_ln1_w': _L0_xcond_in['ln1_w'], 'L0_xcond_ln1_b': _L0_xcond_in['ln1_b'], 'L0_xcond_g1_w': _L0_xcond_in['g1_w'], 'L0_xcond_g1_b': _L0_xcond_in['g1_b'], 'L0_xcond_b1_w': _L0_xcond_in['b1_w'], 'L0_xcond_b1_b': _L0_xcond_in['b1_b'], 'L0_xcond_ln2_w': _L0_xcond_in['ln2_w'], 'L0_xcond_ln2_b': _L0_xcond_in['ln2_b'], 'L0_xcond_g2_w': _L0_xcond_in['g2_w'], 'L0_xcond_g2_b': _L0_xcond_in['g2_b'], 'L0_xcond_b2_w': _L0_xcond_in['b2_w'], 'L0_xcond_b2_b': _L0_xcond_in['b2_b'], 'L0_xcond_sa_wq': _L0_xcond_in['sa_wq'], 'L0_xcond_sa_wkv': _L0_xcond_in['sa_wkv'], 'L0_xcond_sa_wo': _L0_xcond_in['sa_wo'], 'L0_xcond_sa_bo': _L0_xcond_in['sa_bo'], 'L0_xcond_ca_lnc_w': _L0_xcond_in['ca_lnc_w'], 'L0_xcond_ca_lnc_b': _L0_xcond_in['ca_lnc_b'], 'L0_xcond_ca_wq': _L0_xcond_in['ca_wq'], 'L0_xcond_ca_wkv': _L0_xcond_in['ca_wkv'], 'L0_xcond_ca_wo': _L0_xcond_in['ca_wo'], 'L0_xcond_ca_bo': _L0_xcond_in['ca_bo'], 'L0_xcond_ff_w1': _L0_xcond_in['ff_w1'], 'L0_xcond_ff_b1': _L0_xcond_in['ff_b1'], 'L0_xcond_ff_w2': _L0_xcond_in['ff_w2'], 'L0_xcond_ff_b2': _L0_xcond_in['ff_b2']}

def reference(x, cond_1024, ctx_768, L0_xcond_ln1_w, L0_xcond_ln1_b, L0_xcond_g1_w, L0_xcond_g1_b, L0_xcond_b1_w, L0_xcond_b1_b, L0_xcond_ln2_w, L0_xcond_ln2_b, L0_xcond_g2_w, L0_xcond_g2_b, L0_xcond_b2_w, L0_xcond_b2_b, L0_xcond_sa_wq, L0_xcond_sa_wkv, L0_xcond_sa_wo, L0_xcond_sa_bo, L0_xcond_ca_lnc_w, L0_xcond_ca_lnc_b, L0_xcond_ca_wq, L0_xcond_ca_wkv, L0_xcond_ca_wo, L0_xcond_ca_bo, L0_xcond_ff_w1, L0_xcond_ff_b1, L0_xcond_ff_w2, L0_xcond_ff_b2):
    import jax
    import jax.numpy as jnp

    def _L0_xcond_ref(x, cond, context, ln1_w, ln1_b, g1_w, g1_b, b1_w, b1_b, ln2_w, ln2_b, g2_w, g2_b, b2_w, b2_b, sa_wq, sa_wkv, sa_wo, sa_bo, ca_lnc_w, ca_lnc_b, ca_wq, ca_wkv, ca_wo, ca_bo, ff_w1, ff_b1, ff_w2, ff_b2):
        import jax, jax.numpy as jnp
        import numpy as np
        B, N, M = (2, 128, 64)
        D, H, DH = (128, 16, 64)
        MID = H * DH
        DC = 96
        MULT = 4
        EPS = 1e-05

        def _ln(x, w, b):
            mu = jnp.mean(x, -1, keepdims=True)
            var = jnp.mean((x - mu) ** 2, -1, keepdims=True)
            return (x - mu) * jax.lax.rsqrt(var + EPS) * w + b

        def _sincos(n, d):
            inv = 1.0 / 10000.0 ** (jnp.arange(0, d, 2, dtype=jnp.float32) / d)
            ang = jnp.arange(n, dtype=jnp.float32)[:, None] * inv[None, :]
            return (jnp.sin(ang), jnp.cos(ang))

        def _rope(x, sin, cos):
            s = sin[None, None]
            c = cos[None, None]
            xe = x[..., ::2]
            xo = x[..., 1::2]
            re = xe * c - xo * s
            ro = xe * s + xo * c
            return jnp.stack((re, ro), axis=-1).reshape(x.shape)

        def _heads(t):
            b, n, _ = t.shape
            return t.reshape(b, n, H, DH).transpose(0, 2, 1, 3)

        def _attn(xq, ctx, wq, wkv, wo, bo):
            q = _heads(xq @ wq)
            k, v = jnp.split(ctx @ wkv, 2, axis=-1)
            k = _heads(k)
            v = _heads(v)
            sq, cq = _sincos(q.shape[2], DH)
            sk, ck = _sincos(k.shape[2], DH)
            q = _rope(q, sq, cq)
            k = _rope(k, sk, ck)
            sim = jnp.einsum('bhnd,bhmd->bhnm', q, k) * DH ** (-0.5)
            a = jax.nn.softmax(sim, axis=-1)
            o = jnp.einsum('bhnm,bhmd->bhnd', a, v)
            o = o.transpose(0, 2, 1, 3).reshape(xq.shape[0], xq.shape[1], MID)
            return o @ wo + bo

        def _adaln(x, c, lw, lb, gw, gb, bw, bb):
            g = (c @ gw + gb)[:, None, :]
            bt = (c @ bw + bb)[:, None, :]
            return _ln(x, lw, lb) * (1.0 + g) + bt
        attn_in = _adaln(x, cond, ln1_w, ln1_b, g1_w, g1_b, b1_w, b1_b)
        x = _attn(attn_in, attn_in, sa_wq, sa_wkv, sa_wo, sa_bo) + x
        cross_in = _adaln(x, cond, ln1_w, ln1_b, g1_w, g1_b, b1_w, b1_b)
        ctx_n = _ln(context, ca_lnc_w, ca_lnc_b)
        x = _attn(cross_in, ctx_n, ca_wq, ca_wkv, ca_wo, ca_bo) + x
        ffn_in = _adaln(x, cond, ln2_w, ln2_b, g2_w, g2_b, b2_w, b2_b)
        h = jax.nn.gelu(ffn_in @ ff_w1 + ff_b1, approximate=False)
        x = h @ ff_w2 + ff_b2 + x
        return x
    x = _L0_xcond_ref(x, cond_1024, ctx_768, L0_xcond_ln1_w, L0_xcond_ln1_b, L0_xcond_g1_w, L0_xcond_g1_b, L0_xcond_b1_w, L0_xcond_b1_b, L0_xcond_ln2_w, L0_xcond_ln2_b, L0_xcond_g2_w, L0_xcond_g2_b, L0_xcond_b2_w, L0_xcond_b2_b, L0_xcond_sa_wq, L0_xcond_sa_wkv, L0_xcond_sa_wo, L0_xcond_sa_bo, L0_xcond_ca_lnc_w, L0_xcond_ca_lnc_b, L0_xcond_ca_wq, L0_xcond_ca_wkv, L0_xcond_ca_wo, L0_xcond_ca_bo, L0_xcond_ff_w1, L0_xcond_ff_b1, L0_xcond_ff_w2, L0_xcond_ff_b2)
    return x

_drawn_inputs = setup_inputs


def setup_inputs(seed=0):
    import zlib

    import numpy as np

    out = dict(_drawn_inputs(seed))
    spreads = {'L0_xcond_ln1_w': (1.0, 0.6),
     'L0_xcond_ln1_b': (0.0, 0.585),
     'L0_xcond_g1_b': (0.0, 0.8),
     'L0_xcond_b1_b': (0.0, 0.499),
     'L0_xcond_ln2_w': (1.0, 0.6),
     'L0_xcond_ln2_b': (0.0, 0.8),
     'L0_xcond_g2_b': (0.0, 0.8),
     'L0_xcond_b2_b': (0.0, 0.8),
     'L0_xcond_sa_bo': (0.0, 0.1),
     'L0_xcond_ca_lnc_w': (1.0, 0.6),
     'L0_xcond_ca_lnc_b': (0.0, 0.639),
     'L0_xcond_ca_bo': (0.0, 0.1),
     'L0_xcond_ff_b1': (0.0, 0.344),
     'L0_xcond_ff_b2': (0.0, 0.1)}
    factors = {'L0_xcond_g1_w': 8.0,
     'L0_xcond_g2_w': 4.34,
     'L0_xcond_b2_w': 4.523,
     'L0_xcond_sa_wq': 8.0,
     'L0_xcond_ca_wq': 8.0}
    for name, (base, spread) in spreads.items():
        noise = np.random.default_rng([zlib.crc32(name.encode()), seed]).standard_normal(out[name].shape)
        drawn = base * np.exp(spread * noise) if base else spread * noise
        out[name] = jnp.asarray(drawn.astype(out[name].dtype))
    for name, factor in factors.items():
        out[name] = (out[name] * factor).astype(out[name].dtype)
    return out
```

```python
from contextlib import ExitStack

import concourse.bass as bass
import numpy as np
from concourse import mybir

F32 = mybir.dt.float32
F32R = mybir.dt.float32r
ALU = mybir.AluOpType
ACT = mybir.ActivationFunctionType
AX = mybir.AxisListType

D = 128
DH = 64
PAIR = 2 * DH
N = 256
W = 2 * N
EPS = 1e-5
SCALE = DH ** -0.5
STACK2 = 96


class Attention:

    def __init__(self, name, keys, rows, tile, project, maximum):
        self.name, self.keys, self.rows = name, keys, rows
        self.tiles = [(a, min(tile, keys - a)) for a in range(0, keys, tile)]
        self.tile = tile
        self.chunks = [list(range(a, min(a + 2, len(self.tiles)))) for a in range(0, len(self.tiles), 2)]
        self.project = [(a, min(project, keys - a)) for a in range(0, keys, project)]
        n = len(self.project)
        self.groups = [list(range(a, min(a + 2, n))) for a in range(0, n, 2)]
        self.vgroups = [list(range(a, min(a + 4, len(self.tiles)))) for a in range(0, len(self.tiles), 4)]
        self.maxima = [(a, min(maximum, keys - a)) for a in range(0, keys, maximum)]
        if len(self.maxima) > 1 and self.maxima[-1][1] < 8:
            last = self.maxima.pop()
            self.maxima[-1] = (self.maxima[-1][0], self.maxima[-1][1] + last[1])
        self.width = keys + keys % 2
        self.uses = ["q"] + ["k"] * len(self.project) + ["v"] * len(self.vgroups) + \
            ["max"] * (4 * len(self.maxima))


def block_kernel(nc, xT_in, cT_in, ctxT_in, cols_in, cols96_in, ada_in, packs, w1_in, w2_in,
                 rope_in, ident_in, outT):
    T = xT_in.shape[1]
    B = T // N
    M = ctxT_in.shape[1] // B
    DC = ctxT_in.shape[0]
    PAIRS = packs["sa"][0].shape[0]
    STEPS = B * PAIRS
    FF = w1_in.shape[1] // D
    LNC = 512
    NLN = T // LNC
    SA = Attention("sa", N, D, 128, N, N)
    CA = Attention("ca", M, DC, 124, 229, 400)
    CCH = [(a, min(401, M - a)) for a in range(0, M, 401)]
    assert len(CCH) == 4 and PAIRS == 8 and LNC == 2 * N

    with ExitStack() as ctx:
        def sb(name, shape, dt=F32):
            return ctx.enter_context(nc.sbuf_tensor(name, shape, dt))

        def sem(name):
            return ctx.enter_context(nc.semaphore(name))

        xT = sb("xT", [D, T])
        ainT = sb("ainT", [D, T])
        ctxT_all = sb("ctxT_all", [DC, B * M])
        cols = sb("cols", [D, cols_in.shape[1]])
        cols96 = sb("cols96", [DC, 2])
        condT = sb("condT", [D, B])
        ada = sb("ada", [D, 4 * D])
        mod = sb("mod", [D, 4, B])
        modt = sb("modt", [D, 4, B])
        epsc = sb("epsc", [D, 1])
        meanw = sb("meanw", [D, D])
        meanw96 = sb("meanw96", [DC, DC])
        onesw = sb("onesw", [D, DH])
        ident = sb("ident", [D, D])
        rope = sb("rope", [PAIR, 2 * M])
        ropeq = sb("ropeq", [PAIR, 2 * N])

        kv_w = [sb(f"kv_w{i}", [D, 3 * PAIR]) for i in range(2)]
        q_w = [sb(f"q_w{i}", [D, 2 * PAIR]) for i in range(2)]
        o_w = [sb(f"o_w{i}", [PAIR, D]) for i in range(2)]
        src = sb("src", [D, M])
        qsrc = sb("qsrc", [D, N])
        turned = [sb(f"turned{i}", [PAIR, 512]) for i in range(2)]
        krot = sb("krot", [PAIR, CA.width])
        qrot = sb("qrot", [PAIR, N])
        K1 = [sb(f"K1_{i}", [D, 2, CA.width], F32R) for i in range(2)]
        K2 = [sb(f"K2_{i}", [D, 2, CA.width], F32R) for i in range(2)]
        Q1 = [sb(f"Q1_{i}", [D, 2, N], F32R) for i in range(2)]
        Q2 = [sb(f"Q2_{i}", [D, 2, N], F32R) for i in range(2)]
        V = [sb(f"V{i}", [D, len(CA.tiles), PAIR]) for i in range(2)]
        PR = [sb(f"P{i}", [D, 2, W]) for i in range(2)]
        psum_acc = sb("psum_acc", [D, 2, W])
        mx = sb("mx", [D, 4, len(CA.maxima)])
        nmx = sb("nmx", [D, 4])
        oraw = sb("oraw", [PAIR, N])
        rsum = sb("rsum", [PAIR, N])
        oT = sb("oT", [PAIR, N])

        S = [ctx.enter_context(nc.psum_tensor(f"S{i}", [D, 2, W], F32)) for i in range(2)]
        PB = [ctx.enter_context(nc.psum_tensor(f"PB{i}", [D, 512], F32)) for i in range(2)]
        TB = ctx.enter_context(nc.psum_tensor("TB", [D, 512], F32))
        OB = ctx.enter_context(nc.psum_tensor("OB", [D, 512], F32))

        xc = V[0][:, 0:4, :].rearrange("p a b -> p (a b)")
        sq = V[0][:, 4:8, :].rearrange("p a b -> p (a b)")
        sd = V[0][:, 8:12, :].rearrange("p a b -> p (a b)")
        rs = V[1][:, 0:4, :].rearrange("p a b -> p (a b)")
        xh = V[1][:, 4:8, :].rearrange("p a b -> p (a b)")

        w1_sb, w2_sb = PR[0][:, 0, 0:FF * D], PR[1][:, 0, 0:FF * D]

        s_const = sem("constants_loaded")
        s_set = sem("constants_set")
        s_rows = sem("stack_rows_set")
        s_ada_mm = sem("adaln_products")
        s_mod = sem("adaln_vectors")
        s_bias = sem("biases_added")
        s_out = sem("output_stored")
        s_w1 = sem("ff_weights_loaded")

        block = ctx.enter_context(nc.Block())

        class LayerNorm:

            def __init__(self, name):
                self.mean = sem(name + "_mean")
                self.centred = sem(name + "_centred")
                self.squared = sem(name + "_squared")
                self.var = sem(name + "_var")
                self.std = sem(name + "_std")
                self.inv = sem(name + "_inv")
                self.unit = sem(name + "_unit")
                self.done = sem(name + "_done")

        class Steps:

            def __init__(self, a):
                n = a.name
                self.src = sem(n + "_source_loaded")
                self.w = [sem(f"{n}_weights_loaded{i}") for i in range(2)]
                self.wo = [sem(f"{n}_wo_loaded{i}") for i in range(2)]
                self.proj = sem(n + "_projected")
                self.freed = sem(n + "_bank_read")
                self.vread = sem(n + "_v_read")
                self.turned = sem(n + "_turned")
                self.rot = sem(n + "_rotated")
                self.qh = sem(n + "_q_high")
                self.ql = sem(n + "_q_low")
                self.kh = sem(n + "_k_high")
                self.k2 = sem(n + "_k_high2")
                self.kl = sem(n + "_k_low")
                self.mxr = sem(n + "_max_reduced")
                self.mx = sem(n + "_max")
                self.mt = sem(n + "_max_row")
                self.mrow = sem(n + "_max_row_copied")
                self.s = sem(n + "_scores")
                self.e = sem(n + "_exp")
                self.pv = sem(n + "_pv")
                self.acc = sem(n + "_acc")
                self.oev = sem(n + "_o_read")
                self.sum = sem(n + "_sum")
                self.rs = sem(n + "_sum_read")
                self.ot = sem(n + "_o_scaled")
                self.y = sem(n + "_y")
                self.added = sem(n + "_added")

        LN1, LNX, LN2, LN3 = LayerNorm("ln1"), LayerNorm("lnx"), LayerNorm("ln2"), LayerNorm("ln3")
        sems = {"sa": Steps(SA), "ca": Steps(CA)}
        s_ctx = sem("context_loaded")
        s_h = sem("ff_hidden")
        s_g = sem("ff_gelu")
        s_f = sem("ff_out")
        s_y = sem("ff_added")

        def run_steps(eng, body):
            body((0, -1), False, True)
            body((0, 0), True, True)
            body((0, 1), True, True)
            with eng.Fori(1, STEPS // 2 - 1) as i:
                body((i, 0), True, True)
                body((i, 1), True, True)
            body((STEPS // 2 - 1, 0), True, True)
            body((STEPS // 2 - 1, 1), True, False)

        def each_batch(eng, body):
            body(0)
            with eng.Fori(1, B) as b:
                body(b)

        def wait(eng, semaphore, value):
            if not isinstance(value, int) or value > 0:
                eng.wait_ge(semaphore, value)

        def nxt(j):
            return (j[0], j[1] + 1)

        def first_step(J):
            return isinstance(J[0], int) and J == (0, 0)

        def times(j, n):
            return j[0] * (2 * n) + j[1] * n

        def batch(j):
            return (j[0] + j[1] // 2) >> 2

        def slots(a):
            n, u = len(a.chunks), len(a.uses)
            if n == 1:
                return [list(range(u - 2)), list(range(u - 2, u))]
            nk, nv = len(a.project), len(a.vgroups)
            first = [2, 2, 2, 3, 2, 4, 5]
            out, at = [], 0
            for c in range(n):
                k = first[c]
                out.append(list(range(at, at + k)))
                at += k
            out.append(list(range(at, u)))
            assert at < u and at >= 1 + nk + nv
            return out

        @block.sync
        def _(sp):
            for dst, source in ((cols, cols_in), (condT, cT_in), (ada, ada_in), (xT, xT_in),
                                (ropeq, rope_in[:, 2 * M:]), (ident, ident_in), (cols96, cols96_in),
                                (ctxT_all, ctxT_in), (rope, rope_in[:, 0:2 * M])):
                sp.dma_start(dst[:], source).then_inc(s_const, 16)

            def loads(a, s, J, pair):
                kv, wq, wo = packs[a.name]
                if not first_step(J):
                    wait(sp, s.proj, times(J, len(a.uses)) - len(a.uses))
                b = J[1] % 2
                sp.dma_start(kv_w[b][0:a.rows, :], kv[pair]
                             ).then_inc(s.w[b], 16)
                sp.dma_start(q_w[b][:, :], wq[pair]
                             ).then_inc(s.w[b], 16)
                if not first_step(J):
                    wait(sp, s.y, times(J, 1) - 1)
                sp.dma_start(o_w[b][:, :], wo[pair]
                             ).then_inc(s.wo[b], 16)

            def source(a, s, b, first):
                if not first:
                    sp.wait_ge(s.proj, b * (PAIRS * len(a.uses)))
                keys = ainT if a is SA else ctxT_all
                sp.dma_start(src[0:a.rows, 0:a.keys], keys[:, bass.ds(b * a.keys, a.keys)]
                             ).then_inc(s.src, 16)
                sp.dma_start(qsrc[:, :], ainT[:, bass.ds(b * N, N)]).then_inc(s.src, 16)

            for a, ln in ((SA, LN1), (CA, LN2)):
                s = sems[a.name]
                wait(sp, ln.done, 2 * NLN)
                if a is CA:
                    sp.wait_ge(LNX.done, 4 * B)
                source(a, s, 0, True)
                loads(a, s, (0, 0), 0)
                for_each = PAIRS // 2
                for r in range(1, PAIRS):
                    loads(a, s, (0, r), r)
                with sp.Fori(1, B) as b:
                    source(a, s, b, False)
                    for r in range(PAIRS):
                        loads(a, s, (b * for_each, r), r)
            s = sems["ca"]
            sp.wait_ge(s.pv, 1 + len(CA.chunks) * STEPS)
            sp.wait_ge(s.acc, 1 + len(CA.chunks) * STEPS)
            sp.dma_start(w1_sb, w1_in).then_inc(s_w1, 16)
            sp.dma_start(w2_sb, w2_in).then_inc(s_w1, 16)
            for c in range(NLN):
                sp.wait_ge(s_y, c + 1)
                sp.dma_start(outT[:, c * LNC:(c + 1) * LNC], xT[:, c * LNC:(c + 1) * LNC]
                             ).then_inc(s_out, 16)
            sp.wait_ge(s_out, 16 * NLN)


        @block.gpsimd
        def _(pool):
            pool.memset(meanw[:], 1.0 / D).then_inc(s_set, 1)
            pool.memset(meanw96[:], 1.0 / DC).then_inc(s_set, 1)
            pool.memset(onesw[:], 1.0).then_inc(s_set, 1)
            pool.memset(epsc[:], EPS).then_inc(s_set, 1)
            pool.memset(psum_acc[:], 0.0).then_inc(sems["ca"].acc, 1)

            a, s = CA, sems["ca"]
            n, rows = len(a.chunks), a.tile

            def body(j, attn, prep):
                if not attn:
                    return
                for c in range(1, n):
                    wait(pool, s.e, 1 + times(j, n) + c + 1)
                    if c == 1:
                        wait(pool, s.sum, times(j, 1))
                    else:
                        wait(pool, s.acc, times(j, n) + c + 1)
                    P = PR[(j[1] * n + c) % 2]
                    if c == 1:
                        ins = pool.tensor_tensor(psum_acc[0:rows], PR[(j[1] * n) % 2][0:rows], P[0:rows],
                                                 ALU.add)
                        ins.then_inc(s.acc, 2)
                    elif len(a.chunks[c]) == 2:
                        pool.tensor_tensor(psum_acc[0:rows], psum_acc[0:rows], P[0:rows], ALU.add
                                           ).then_inc(s.acc, 1)
                    else:
                        last = a.tiles[-1][1]
                        pool.tensor_tensor(psum_acc[0:last, 0], psum_acc[0:last, 0], P[0:last, 0], ALU.add
                                           ).then_inc(s.acc, 1)

            run_steps(pool, body)

        @block.scalar
        def _(act):
            def copy(out, in_):
                return act.activation(out, in_, ACT.Copy)

            def norm(ln, c, sq_, xc_, pb_, sd_, eps_):
                wait(act, ln.centred, c + 1)
                wait(act, ln.var, c)
                act.activation(sq_, xc_, ACT.Square).then_inc(ln.squared, 1)
                wait(act, ln.var, c + 1)
                wait(act, ln.inv, c)
                act.activation(sd_, pb_, ACT.Sqrt, bias=eps_).then_inc(ln.std, 1)

            def attention(a, s):
                n, nk, nv = len(a.chunks), len(a.project), len(a.vgroups)

                def piece(J, u):
                    b = J[1] % 2
                    kind = a.uses[u]
                    if kind == "q":
                        wait(act, s.rot, times(J, 1 + nk) + 1)
                        if not first_step(J):
                            wait(act, s.s, times(J, n) - n)
                            wait(act, s.y, times(J, 1) - 1)
                        for h in range(2):
                            for half in range(2):
                                ins = copy(Q1[b][half * DH:(half + 1) * DH, h, :],
                                           qrot[h * DH:(h + 1) * DH, :])
                        ins.then_inc(s.qh, 1)
                    if kind == "k":
                        k = u - 1
                        for g, group in enumerate(a.groups):
                            if group[-1] != k:
                                continue
                            lo = a.project[group[0]][0]
                            hi = a.project[k][0] + a.project[k][1]
                            wait(act, s.rot, times(J, 1 + nk) + 2 + k)
                            if not first_step(J) and g == 0:
                                wait(act, s.s, times(J, n) - n)
                            for h in range(2):
                                ins = copy(K1[b][h * DH:(h + 1) * DH, h, lo:hi],
                                           krot[h * DH:(h + 1) * DH, lo:hi])
                            ins.then_inc(s.kh, 1)
                            for h in range(2):
                                ins = copy(K2[b][0:DH, h, lo:hi], krot[h * DH:(h + 1) * DH, lo:hi])
                            ins.then_inc(s.k2, 1)
                    if kind == "v":
                        v = u - 1 - nk
                        wait(act, s.proj, times(J, len(a.uses)) + u + 1)
                        if not first_step(J) and v == 0:
                            wait(act, s.pv, 1 + times(J, n) - n)
                        g = a.vgroups[v]
                        PBu = PB[(J[1] * len(a.uses) + u) % 2]
                        full = [t for t in g if a.tiles[t][1] == a.tile]
                        if full:
                            ins = copy(V[b][0:a.tile, full[0]:full[-1] + 1, :],
                                       PBu[0:a.tile, 0:len(full) * PAIR].rearrange("p (t n) -> p t n", n=PAIR))
                        for t in g:
                            if a.tiles[t][1] < a.tile:
                                k0 = (t - g[0]) * PAIR
                                ins = copy(V[b][0:a.tiles[t][1], t, :], PBu[0:a.tiles[t][1], k0:k0 + PAIR])
                        ins.then_inc(s.vread, 1)

                def body(j, attn, prep):
                    J = nxt(j)
                    for c, us in enumerate(slots(a)):
                        if attn and c < n:
                            rows = a.tiles[a.chunks[c][0]][1]
                            k = len(a.chunks[c])
                            i = (j[1] * n + c) % 2
                            wait(act, s.s, times(j, n) + c + 1)
                            wait(act, s.pv, times(j, n) + c)
                            if a is CA:
                                wait(act, s.acc, times(j, n) + c)
                            else:
                                wait(act, s.sum, times(j, 1))
                            act.activation(PR[i][0:rows, 0:k], S[i][0:rows, 0:k], ACT.Exp, scale=SCALE
                                           ).then_inc(s.e, 1)
                        if prep:
                            for u in us:
                                piece(J, u)

                run_steps(act, body)

            act.wait_ge(s_set, 4)
            act.activation(nmx[:, 0:1], epsc[:, :], ACT.Exp).then_inc(sems["sa"].e, 1)
            act.wait_ge(sems["sa"].e, 1)
            act.activation(nmx[:, 0:1], epsc[:, :], ACT.Exp).then_inc(sems["ca"].e, 1)
            for c in range(NLN):
                norm(LN1, c, sq, xc, PB[1][:, :], sd, epsc[:, :])
            attention(SA, sems["sa"])
            for c in range(NLN):
                norm(LN2, c, sq, xc, PB[1][:, :], sd, epsc[:, :])
            def context_norm(b):
                for i, (lo, n) in enumerate(CCH):
                    norm(LNX, b * 4 + i, sq[0:DC, 0:n], xc[0:DC, 0:n], PB[1][0:DC, 0:n],
                         sd[0:DC, 0:n], epsc[0:DC, :])

            each_batch(act, context_norm)
            attention(CA, sems["ca"])
            for c in range(NLN):
                norm(LN3, c, sq, xc, PB[1][:, :], sd, epsc[:, :])
            for c in range(NLN):
                for f in range(FF):
                    n = c * FF + f
                    act.wait_ge(s_h, n + 1)
                    if n >= 2:
                        act.wait_ge(s_f, n - 1)
                    act.activation(turned[n % 2][:, :], S[n % 2][:, 0, :], ACT.Gelu,
                                   bias=cols[:, 12 + f:13 + f]).then_inc(s_g, 1)

        @block.vector
        def _(dve):
            def adaln_vectors():
                dve.wait_ge(s_ada_mm, 1)
                n = 0
                for i in range(2):
                    dve.tensor_scalar(modt[:, 2 * i, :], OB[:, 16 * i:16 * i + B], cols[:, 4 * i + 2:4 * i + 3],
                                      1.0, ALU.add, ALU.add).then_inc(s_mod, 1)
                    dve.tensor_scalar(modt[:, 2 * i + 1, :], OB[:, 16 * i + 8:16 * i + 8 + B],
                                      cols[:, 4 * i + 3:4 * i + 4], None, ALU.add).then_inc(s_mod, 1)
                    n += 2
                    dve.wait_ge(s_mod, n)
                    dve.tensor_scalar(mod[:, 2 * i, :], modt[:, 2 * i, :], cols[:, 4 * i:4 * i + 1], None,
                                      ALU.mult).then_inc(s_mod, 1)
                    dve.scalar_tensor_tensor(out=mod[:, 2 * i + 1, :], in0=modt[:, 2 * i, :],
                                             scalar=cols[:, 4 * i + 1:4 * i + 2], in1=modt[:, 2 * i + 1, :],
                                             op0=ALU.mult, op1=ALU.add).then_inc(s_mod, 1)
                    n += 2
                dve.wait_ge(s_mod, n)

            def norm(ln, c, x_, xc_, pb_, sd_, rs_, xh_):
                wait(dve, ln.mean, c + 1)
                wait(dve, ln.squared, c)
                wait(dve, ln.unit, c)
                dve.tensor_tensor(xc_, x_, pb_, ALU.subtract).then_inc(ln.centred, 1)
                wait(dve, ln.std, c + 1)
                dve.reciprocal(rs_, sd_).then_inc(ln.inv, 1)
                wait(dve, ln.inv, c + 1)
                dve.tensor_tensor(xh_, xc_, rs_, ALU.mult).then_inc(ln.unit, 1)
                wait(dve, ln.unit, c + 1)

            def adaln(ln, i):
                for c in range(NLN):
                    norm(ln, c, xT[:, c * LNC:(c + 1) * LNC], xc, PB[0][:, :], sd, rs, xh)
                    for h in range(2):
                        b = 2 * c + h
                        ins = dve.tensor_scalar(ainT[:, b * N:(b + 1) * N], xh[:, h * N:(h + 1) * N],
                                                mod[:, 2 * i, b:b + 1], mod[:, 2 * i + 1, b:b + 1],
                                                ALU.mult, ALU.add)
                        ins.then_inc(ln.done, 1)

            def add_bias(k, n):
                dve.tensor_scalar(xT[:, :], xT[:, :], cols[:, k:k + 1], None, ALU.add).then_inc(s_bias, 1)
                dve.wait_ge(s_bias, n)

            def attention(a, s):
                n, nk, nu, nm = len(a.chunks), len(a.project), len(a.uses), len(a.maxima)
                nfree = 1 + nk + 4 * nm
                table = ropeq if a is SA else rope

                def piece(J, u):
                    b = J[1] % 2
                    kind = a.uses[u]
                    if kind == "v":
                        return
                    PBu = PB[(J[1] * nu + u) % 2]
                    if kind == "max" and u == 1 + nk + len(a.vgroups):
                        low_group(J, len(a.groups) - 1)
                    wait(dve, s.proj, times(J, nu) + u + 1)
                    if kind == "q":
                        dve.tensor_tensor(turned[0][:, :], PBu[:, :], ropeq[:, :], ALU.mult
                                          ).then_inc(s.freed, 1)
                        wait(dve, s.freed, times(J, nfree) + 1)
                        if not first_step(J):
                            wait(dve, s.qh, times(J, 1))
                            wait(dve, s.ql, times(J, 1))
                        dve.tensor_tensor(qrot[:, :], turned[0][:, 0:N], turned[0][:, N:2 * N], ALU.add
                                          ).then_inc(s.rot, 1)
                        wait(dve, s.qh, times(J, 1) + 1)
                        for h in range(2):
                            ins = dve.tensor_tensor(Q2[b][0:DH, h, :], qrot[h * DH:(h + 1) * DH, :],
                                                    Q1[b][h * DH:(h + 1) * DH, h, :].bitcast(F32),
                                                    ALU.subtract)
                        ins.then_inc(s.ql, 1)
                    if kind == "k":
                        k = u - 1
                        lo, w = a.project[k]
                        i = (k + 1) % 2
                        if k >= 1 or True:
                            wait(dve, s.rot, times(J, 1 + nk) + (k + 1 if k else 1))
                        dve.tensor_tensor(turned[i][:, 0:2 * w], PBu[:, 0:2 * w],
                                          table[:, 2 * lo:2 * (lo + w)], ALU.mult).then_inc(s.freed, 1)
                        wait(dve, s.freed, times(J, nfree) + 2 + k)
                        if not first_step(J) and k == 0:
                            wait(dve, s.k2, times(J, len(a.groups)))
                            wait(dve, s.kl, times(J, len(a.groups)))
                        dve.tensor_tensor(krot[:, lo:lo + w], turned[i][:, 0:w], turned[i][:, w:2 * w],
                                          ALU.add).then_inc(s.rot, 1)
                        low(J, k)
                    if kind == "max":
                        m = u - 1 - nk - len(a.vgroups)
                        if m == 0:
                            if not first_step(J):
                                wait(dve, s.mx, times(J, 1))
                        hq, c = m // nm, m % nm
                        dve.tensor_reduce(mx[:, hq, c:c + 1], PBu[:, 0:a.maxima[c][1]], AX.X, ALU.max
                                          ).then_inc(s.freed, 1)

                def low(J, k):
                    for g in range(1, len(a.groups)):
                        if a.groups[g][-1] == k:
                            low_group(J, g - 1)

                def low_group(J, g):
                    b = J[1] % 2
                    group = a.groups[g]
                    lo = a.project[group[0]][0]
                    hi = a.project[group[-1]][0] + a.project[group[-1]][1]
                    wait(dve, s.kh, times(J, len(a.groups)) + g + 1)
                    for h in range(2):
                        o = (1 - h) * DH
                        ins = dve.tensor_tensor(K1[b][o:o + DH, h, lo:hi], krot[h * DH:(h + 1) * DH, lo:hi],
                                                K1[b][h * DH:(h + 1) * DH, h, lo:hi].bitcast(F32),
                                                ALU.subtract)
                    ins.then_inc(s.kl, 1)

                def body(j, attn, prep):
                    J = nxt(j)
                    plan = slots(a)
                    for us in plan[:-1]:
                        if prep:
                            for u in us:
                                piece(J, u)
                    if attn:
                        wait(dve, s.pv, 1 + times(j, n) + n)
                        wait(dve, s.ot, times(j, 1))
                        dve.tensor_copy(oraw[:, :], OB[:, 0:N]).then_inc(s.oev, 1)
                    if prep:
                        for u in plan[-1]:
                            piece(J, u)
                        wait(dve, s.freed, times(J, nfree) + nfree)
                        if not first_step(J):
                            wait(dve, s.mt, times(J, 1))
                        dve.tensor_reduce(nmx[:, :], mx[:, :, 0:nm], AX.X, ALU.max, negate=True
                                          ).then_inc(s.mx, 1)
                    if attn:
                        wait(dve, s.sum, times(j, 1) + 1)
                        dve.reciprocal(rsum[:, :], TB[:, 0:N]).then_inc(s.rs, 1)
                        wait(dve, s.rs, times(j, 1) + 1)
                        wait(dve, s.oev, times(j, 1) + 1)
                        wait(dve, s.y, times(j, 1))
                        dve.tensor_tensor(oT[:, :], oraw[:, :], rsum[:, :], ALU.mult).then_inc(s.ot, 1)
                    if prep:
                        wait(dve, s.mt, times(J, 1) + 1)
                        if not first_step(J):
                            wait(dve, s.s, times(J, n) - n)
                        dve.tensor_copy(Q2[J[1] % 2][DH:DH + 1].rearrange("p h n -> p (h n)"),
                                        TB[DH:DH + 1, :]).then_inc(s.mrow, 1)
                    if attn:
                        wait(dve, s.y, times(j, 1) + 1)
                        wait(dve, s.added, times(j, 1))
                        b = nc.s_assert_within(batch(j), 0, B - 1, skip_runtime_bounds_check_because=
                                               "there are PAIRS steps for each of the B batches")
                        dve.tensor_tensor(xT[:, bass.ds(b * N, N)], xT[:, bass.ds(b * N, N)], TB[:, 0:N],
                                          ALU.add).then_inc(s.added, 1)

                run_steps(dve, body)
                dve.wait_ge(s.added, STEPS)

            for i in range(2):
                dve.memset(K2[i][DH:STACK2].bitcast(F32), 0.0).then_inc(s_rows, 1)
                dve.memset(Q2[i][DH:STACK2].bitcast(F32), 0.0).then_inc(s_rows, 1)
                dve.memset(K1[i][:, :, CA.keys:CA.width].bitcast(F32), 0.0).then_inc(s_rows, 1)
            dve.wait_ge(s_rows, 6)
            for i in range(2):
                dve.memset(K2[i][DH:DH + 1].bitcast(F32), 1.0).then_inc(s_rows, 1)
            dve.wait_ge(s_rows, 8)
            dve.wait_ge(s_const, 16 * 9)
            dve.wait_ge(s_set, 4)
            adaln_vectors()
            adaln(LN1, 0)
            add_bias(8, 1)
            attention(SA, sems["sa"])
            adaln(LN2, 0)
            add_bias(9, 2)
            def context_norm(b):
                for i, (lo, n) in enumerate(CCH):
                    x_ = ctxT_all[:, bass.ds(b * M + lo, n)]
                    norm(LNX, b * 4 + i, x_, xc[0:DC, 0:n], PB[0][0:DC, 0:n], sd[0:DC, 0:n],
                         rs[0:DC, 0:n], xh[0:DC, 0:n])
                    dve.tensor_scalar(x_, xh[0:DC, 0:n], cols96[:, 0:1], cols96[:, 1:2], ALU.mult, ALU.add
                                      ).then_inc(LNX.done, 1)

            each_batch(dve, context_norm)
            attention(CA, sems["ca"])
            adaln(LN3, 1)
            add_bias(10, 3)
            for c in range(NLN):
                dve.wait_ge(s_f, (c + 1) * FF)
                dve.tensor_tensor(xT[:, c * LNC:(c + 1) * LNC], xT[:, c * LNC:(c + 1) * LNC],
                                  PB[c % 2][:, :], ALU.add).then_inc(s_y, 1)

        @block.tensor
        def _(pe):
            def norm(ln, c, x_, xc_unused, w, pb0, pb1, sq_):
                wait(pe, ln.centred, c)
                pe.matmul(pb0, w, x_, start=True, stop=True).then_inc(ln.mean, 1)
                wait(pe, ln.squared, c + 1)
                wait(pe, ln.std, c)
                pe.matmul(pb1, w, sq_, start=True, stop=True).then_inc(ln.var, 1)

            def norm_x(ln):
                for c in range(NLN):
                    norm(ln, c, xT[:, c * LNC:(c + 1) * LNC], None, meanw[:, :], PB[0][:, :], PB[1][:, :], sq)

            def attention(a, s):
                n, nk, nu, nm = len(a.chunks), len(a.project), len(a.uses), len(a.maxima)
                nv = len(a.vgroups)
                nfree = 1 + nk + 4 * nm
                order, count = [], {"v": 0, "d": 0}
                for kind in a.uses:
                    who = "v" if kind == "v" else "d"
                    order.append((who, count[who]))
                    count[who] += 1

                def bank_free(J, u):
                    first = u < 2
                    who, k = order[(u - 2) % nu]
                    if first and first_step(J):
                        return
                    back = times(J, nfree if who == "d" else nv) + k + 1
                    if first:
                        back = back - (nfree if who == "d" else nv)
                    pe.wait_ge(s.freed if who == "d" else s.vread, back)

                def piece(J, u):
                    b = J[1] % 2
                    kind = a.uses[u]
                    PBu = PB[(J[1] * nu + u) % 2]
                    bank_free(J, u)
                    if kind == "q":
                        pe.wait_ge(s.w[b], (J[0] + J[1] // 2) * 32 + 32)
                        pe.wait_ge(s.src, batch(J) * 32 + 32)
                        for i in range(2):
                            ins = pe.matmul(PBu[:, i * N:(i + 1) * N], q_w[b][:, i * PAIR:(i + 1) * PAIR],
                                            qsrc[:, :], start=True, stop=True)
                    if kind == "k":
                        lo, w = a.project[u - 1]
                        for i in range(2):
                            ins = pe.matmul(PBu[:, i * w:(i + 1) * w],
                                            kv_w[b][0:a.rows, i * PAIR:(i + 1) * PAIR],
                                            src[0:a.rows, lo:lo + w], start=True, stop=True)
                    if kind == "v":
                        g = a.vgroups[u - 1 - nk]
                        for t in g:
                            lo, w = a.tiles[t]
                            k0 = (t - g[0]) * PAIR
                            ins = pe.matmul(PBu[0:w, k0:k0 + PAIR], src[0:a.rows, lo:lo + w],
                                            kv_w[b][0:a.rows, 2 * PAIR:3 * PAIR], start=True, stop=True)
                    if kind == "max":
                        m = u - 1 - nk - nv
                        hq, c = m // nm, m % nm
                        h, qt = hq // 2, hq % 2
                        lo, w = a.maxima[c]
                        if m == 0:
                            wait(pe, s.qh, times(J, 1) + 1)
                            wait(pe, s.kh, times(J, len(a.groups)) + len(a.groups))
                            wait(pe, s.kl, times(J, len(a.groups)) + len(a.groups))
                        w += w % 2
                        ins = pe.matmul(PBu[:, 0:w], Q1[b][:, h, qt * 128:(qt + 1) * 128],
                                        K1[b][:, h, lo:lo + w], start=True, stop=True)
                    ins.then_inc(s.proj, 1)

                def scores(j, c):
                    b, i = j[1] % 2, (j[1] * n + c) % 2
                    if c == 0:
                        wait(pe, s.k2, times(j, len(a.groups)) + len(a.groups))
                        wait(pe, s.ql, times(j, 1) + 1)
                        wait(pe, s.mrow, times(j, 1) + 1)
                    wait(pe, s.e, times(j, n) + c)
                    for k, t in enumerate(a.chunks[c]):
                        lo, w = a.tiles[t]
                        for h in range(2):
                            out = S[i][0:w, k, h * N:(h + 1) * N]
                            pe.matmul(out, K1[b][:, h, lo:lo + w], Q1[b][:, h, :], start=True, stop=False)
                            ins = pe.matmul(out, K2[b][0:STACK2, h, lo:lo + w], Q2[b][0:STACK2, h, :],
                                            start=False, stop=True)
                    ins.then_inc(s.s, 1)

                def products(j, c):
                    b, i = j[1] % 2, (j[1] * n + c) % 2
                    if c == 0:
                        wait(pe, s.vread, times(j, nv) + nv)
                        wait(pe, s.oev, times(j, 1))
                    wait(pe, s.e, 1 + times(j, n) + c + 1)
                    for k, t in enumerate(a.chunks[c]):
                        w = a.tiles[t][1]
                        for h in range(2):
                            ins = pe.matmul(OB[h * DH:(h + 1) * DH, 0:N], V[b][0:w, t, h * DH:(h + 1) * DH],
                                            PR[i][0:w, k, h * N:(h + 1) * N], start=(t == 0),
                                            stop=(t == len(a.tiles) - 1))
                    ins.then_inc(s.pv, 1)

                def sums(j):
                    wait(pe, s.added, times(j, 1))
                    if a is CA:
                        wait(pe, s.acc, 1 + times(j, n) + n)
                        source = psum_acc
                    else:
                        source = PR[j[1] % 2]
                    rows = a.tile
                    for h in range(2):
                        for k in range(2):
                            ins = pe.matmul(TB[h * DH:(h + 1) * DH, 0:N], onesw[0:rows, :],
                                            source[0:rows, k, h * N:(h + 1) * N], start=(k == 0),
                                            stop=(k == 1))
                    ins.then_inc(s.sum, 1)

                def max_row(J, attn):
                    wait(pe, s.mx, times(J, 1) + 1)
                    if attn:
                        wait(pe, s.rs, times(J, 1))
                    for hq in range(4):
                        ins = pe.matmul(TB[DH:DH + 1, hq * 128:(hq + 1) * 128], nmx[:, hq:hq + 1],
                                        ident[:, :], start=True, stop=True)
                    ins.then_inc(s.mt, 1)

                def output(j, prep):
                    b = j[1] % 2
                    pe.wait_ge(s.wo[b], (j[0] + j[1] // 2) * 16 + 16)
                    wait(pe, s.ot, times(j, 1) + 1)
                    if prep:
                        wait(pe, s.mrow, times(j, 1) + 2)
                    else:
                        wait(pe, s.rs, times(j, 1) + 1)
                    pe.matmul(TB[:, 0:N], o_w[b][:, :], oT[:, :], start=True, stop=True).then_inc(s.y, 1)

                def body(j, attn, prep):
                    J = nxt(j)
                    plan = slots(a)
                    if attn:
                        scores(j, 0)
                    for c in range(n):
                        if attn and c + 1 < n:
                            scores(j, c + 1)
                        if prep:
                            for u in plan[c]:
                                piece(J, u)
                        if attn:
                            products(j, c)
                    if prep:
                        for u in plan[-1]:
                            piece(J, u)
                    if attn:
                        sums(j)
                    if prep:
                        max_row(J, attn)
                    if attn:
                        output(j, prep)

                run_steps(pe, body)

            pe.wait_ge(s_const, 16 * 9)
            pe.wait_ge(s_set, 4)
            for i in range(4):
                ins = pe.matmul(OB[:, 8 * i:8 * i + B], ada[:, i * D:(i + 1) * D], condT[:, :], start=True,
                                stop=True)
            ins.then_inc(s_ada_mm, 1)
            pe.matmul(TB[:, 0:B], ident[:, :], condT[:, :], start=True, stop=True
                      ).then_inc(sems["sa"].pv, 1)
            pe.matmul(TB[:, 0:B], ident[:, :], condT[:, :], start=True, stop=True
                      ).then_inc(sems["ca"].pv, 1)
            pe.wait_ge(s_mod, 8)
            norm_x(LN1)
            attention(SA, sems["sa"])
            pe.wait_ge(sems["sa"].added, STEPS)
            norm_x(LN2)
            def context_norm(b):
                for i, (lo, n) in enumerate(CCH):
                    norm(LNX, b * 4 + i, ctxT_all[:, bass.ds(b * M + lo, n)], None,
                         meanw96[:, :], PB[0][0:DC, 0:n], PB[1][0:DC, 0:n], sq[0:DC, 0:n])

            each_batch(pe, context_norm)
            attention(CA, sems["ca"])
            pe.wait_ge(sems["ca"].added, STEPS)
            norm_x(LN3)
            pe.wait_ge(s_w1, 32)
            for c in range(NLN):
                pe.wait_ge(LN3.done, 2 * (c + 1))
                if c == 0:
                    pe.wait_ge(LN3.done, 2 * NLN)
                if c >= 2:
                    pe.wait_ge(s_y, c - 1)

                def hidden(c, f):
                    n = c * FF + f
                    if n >= 2:
                        pe.wait_ge(s_g, n - 1)
                    pe.matmul(S[n % 2][:, 0, :], w1_sb[:, f * D:(f + 1) * D], ainT[:, c * LNC:(c + 1) * LNC],
                              start=True, stop=True).then_inc(s_h, 1)

                if c == 0:
                    hidden(0, 0)
                for f in range(FF):
                    n = c * FF + f
                    if n + 1 < NLN * FF:
                        hidden((n + 1) // FF, (n + 1) % FF)
                    pe.wait_ge(s_g, n + 1)
                    pe.matmul(PB[c % 2][:, :], w2_sb[:, f * D:(f + 1) * D], turned[n % 2][:, :],
                              start=(f == 0), stop=(f == FF - 1)).then_inc(s_f, 1)


def kernel(**inputs):
    import concourse.bacc as bacc
    from concourse.bass_utils import run_bass_kernel_spmd

    a = {k.removeprefix("L0_xcond_"): np.asarray(v) for k, v in inputs.items()}
    B, n, D_ = a["x"].shape
    M = a["ctx_768"].shape[1]
    pairs = a["sa_wq"].shape[1] // PAIR

    def halves(w, swap):
        w = w.reshape(w.shape[0], pairs, 2, DH // 2, 2)
        w = w[..., ::-1] if swap else w
        return w.transpose(1, 0, 2, 4, 3).reshape(pairs, w.shape[0], PAIR)

    def packs(p):
        wk, wv = np.split(a[p + "_wkv"], 2, axis=1)
        wv = wv.reshape(wv.shape[0], pairs, PAIR).transpose(1, 0, 2)
        kv = np.concatenate([halves(wk, False), halves(wk, True), wv], axis=2)
        wq = a[p + "_wq"]
        return kv, np.concatenate([halves(wq, False), halves(wq, True)], axis=2), \
            a[p + "_wo"].reshape(pairs, PAIR, D_)

    inv = (np.float32(1) / np.float32(10000) ** (np.arange(0, DH, 2, dtype=np.float32) / np.float32(DH))
           ).astype(np.float32)
    ang = np.arange(M, dtype=np.float32)[:, None] * inv[None, :]
    cos, sin = np.cos(ang).T, np.sin(ang).T
    C = np.concatenate([cos] * 4, 0)
    Sg = np.concatenate([-sin, sin] * 2, 0)

    def interleave(keys, chunk):
        out = []
        for lo in range(0, keys, chunk):
            hi = min(lo + chunk, keys)
            out += [C[:, lo:hi], Sg[:, lo:hi]]
        return out

    rope = np.concatenate(interleave(M, 229) + interleave(n, n), axis=1)
    ff = a["ff_w1"].shape[1] // D_
    cols = np.stack([a["ln1_w"], a["ln1_b"], a["g1_b"], a["b1_b"], a["ln2_w"], a["ln2_b"], a["g2_b"],
                     a["b2_b"], a["sa_bo"], a["ca_bo"], a["ff_b2"], a["ff_b2"]]
                    + list(a["ff_b1"].reshape(ff, D_)), axis=1)
    arrays = {
        "xT": a["x"].transpose(2, 0, 1).reshape(D_, B * n),
        "condT": a["cond_1024"].T,
        "ctxT": a["ctx_768"].transpose(2, 0, 1).reshape(-1, B * M),
        "cols": cols,
        "cols96": np.stack([a["ca_lnc_w"], a["ca_lnc_b"]], axis=1),
        "ada": np.concatenate([a["g1_w"], a["b1_w"], a["g2_w"], a["b2_w"]], axis=1),
        "w1": a["ff_w1"],
        "w2": a["ff_w2"].reshape(ff, D_, D_).transpose(1, 0, 2).reshape(D_, ff * D_),
        "rope": rope,
        "ident": np.eye(D_, dtype=np.float32),
    }
    for p in ("sa", "ca"):
        for name, w in zip(("kv", "wq", "wo"), packs(p)):
            arrays[f"{p}_{name}"] = w
    arrays = {k: np.ascontiguousarray(v) for k, v in arrays.items()}

    nc = bacc.Bacc("TRN2", target_bir_lowering=False, num_devices=1)
    t = {k: nc.dram_tensor(k + "_dram", v.shape, F32, kind="ExternalInput").ap() for k, v in arrays.items()}
    out = nc.dram_tensor("outT_dram", (D_, B * n), F32, kind="ExternalOutput").ap()
    block_kernel(nc, t["xT"], t["condT"], t["ctxT"], t["cols"], t["cols96"], t["ada"],
                 {p: (t[p + "_kv"], t[p + "_wq"], t[p + "_wo"]) for p in ("sa", "ca")},
                 t["w1"], t["w2"], t["rope"], t["ident"], out)
    r = run_bass_kernel_spmd(nc, [{k + "_dram": v for k, v in arrays.items()}], core_ids=[0])
    return r.results[0]["outT_dram"].reshape(D_, B, n).transpose(1, 2, 0)
```

```python
from contextlib import ExitStack

import concourse.bass as bass
import numpy as np
from concourse import mybir

F32 = mybir.dt.float32
F32R = mybir.dt.float32r
ALU = mybir.AluOpType
ACT = mybir.ActivationFunctionType
AX = mybir.AxisListType

D = 128
DH = 64
PAIR = 2 * DH
N = 256
W = 2 * N
EPS = 1e-5
SCALE = DH ** -0.5
UNROLL = 4
STACK2 = 96


class Attention:

    def __init__(self, name, keys, rows, tile, project, maximum, lead, pe, dve, act):
        self.name, self.keys, self.rows, self.tile, self.lead = name, keys, rows, tile, lead
        self.pe, self.dve, self.act = ([(w.rstrip("0123456789"), int("0" + w.lstrip("abcdefghijklmnopqrstuvwxyzSEPM")))
                                        for w in text.split()] for text in (pe, dve, act))
        self.tiles = [(a, min(tile, keys - a)) for a in range(0, keys, tile)]
        self.chunks = [list(range(a, min(a + 2, len(self.tiles)))) for a in range(0, len(self.tiles), 2)]
        self.project = [(a, min(project, keys - a)) for a in range(0, keys, project)]
        n = len(self.project)
        self.groups = [list(range(a, min(a + 2, n))) for a in range(0, n, 2)]
        self.vgroups = [list(range(a, min(a + 4, len(self.tiles)))) for a in range(0, len(self.tiles), 4)]
        self.maxima = [(a, maximum) for a in range(0, keys - maximum + 1, maximum)]
        self.maxima[-1] = (self.maxima[-1][0], keys - self.maxima[-1][0])
        self.width = keys + keys % 2
        self.ring = 2 * lead
        uses = [w for w in self.pe if w[0] in ("q", "k", "v", "a")]
        self.bank = {w: i % 2 if lead == 1 else int(w[0] == "a") for i, w in enumerate(uses)}
        self.before = {}
        for w in uses:
            same = [v for v in uses if self.bank[v] == self.bank[w]]
            self.before[w] = (same[same.index(w) - 1], int(w == same[0]))
        self.count = {"proj": [w for w in uses if w[0] != "a"], "a": [w for w in uses if w[0] == "a"],
                      "v": [w for w in uses if w[0] == "v"], "qk": [w for w in uses if w[0] in "qk"]}


def block_kernel(nc, xT_in, cT_in, ctxT_in, cols_in, cols96_in, ada_in, packs, w1_in, w2_in,
                 rope_in, ident_in, outT):
    T = xT_in.shape[1]
    B = T // N
    M = ctxT_in.shape[1] // B
    DC = ctxT_in.shape[0]
    PAIRS = packs["sa"][0].shape[0]
    STEPS = B * PAIRS
    FF = w1_in.shape[1] // D
    LNC = 512
    NLN = T // LNC
    CLN = 402
    NCL = 32
    SELF = Attention("sa", N, D, 128, N, N, 2,
                      "q sum a0 v0 a1 k0 S0 M P0 out",
                      "q a0 div a1 k0 row ql oev add l0",
                      "v0 q E0 g0")
    CROSS = Attention("ca", M, DC, 124, 229, 400, 1,
                      "q k0 k1 S0 k2 k3 sum v0 k4 S1 a0 a1 P0 v1 P1 a2 a3 S2 k5 S3 k6 a4 P2 a5 P3 a6 "
                      "out a7 S4 a8 a9 S5 a10 a11 P4 a12 S6 a13 a14 P5 a15 v2 P6 v3 M",
                      "q k0 k1 k2 k3 l0 k4 a0 a1 div a2 a3 l1 k5 k6 a4 a5 l2 a6 a7 a8 a9 l3 a10 a11 "
                      "a12 a13 a14 add a15 mx ql oev row",
                      "q E0 g0 v0 g1 E1 v1 E2 E3 g2 g3 E4 E5 E6 v2 v3")
    assert PAIRS == 2 * UNROLL and LNC == 2 * N and NCL * CLN >= B * M

    with ExitStack() as ctx:
        def sb(name, shape, dt=F32):
            return ctx.enter_context(nc.sbuf_tensor(name, shape, dt))

        def sem(name):
            return ctx.enter_context(nc.semaphore(name))

        xT = sb("xT", [D, T])
        ainT = sb("ainT", [D, T])
        ctxT_all = sb("ctxT_all", [DC, NCL * CLN])
        cols = sb("cols", [D, cols_in.shape[1]])
        cols96 = sb("cols96", [DC, 2])
        condT = sb("condT", [D, B])
        ada = sb("ada", [D, 4 * D])
        mod = sb("mod", [D, 4, B])
        modt = sb("modt", [D, 4, B])
        epsc = sb("epsc", [D, 1])
        meanw = sb("meanw", [D, D])
        meanw96 = sb("meanw96", [DC, DC])
        onesw = sb("onesw", [D, DH])
        ident = sb("ident", [D, D])
        rope = sb("rope", [PAIR, 2 * M])
        ropeq = sb("ropeq", [PAIR, 2 * N])

        kv_w = [sb(f"kv_w{i}", [D, 3 * PAIR]) for i in range(2)]
        q_w = [sb(f"q_w{i}", [D, 2 * PAIR]) for i in range(2)]
        o_w = [sb(f"o_w{i}", [PAIR, D]) for i in range(UNROLL)]
        src = sb("src", [D, M])
        qsrc = sb("qsrc", [D, N])
        turned = [sb(f"turned{i}", [PAIR, 512]) for i in range(2)]
        krot = sb("krot", [PAIR, CROSS.width])
        qrot = sb("qrot", [PAIR, N])
        K1b = [sb(f"K1_{i}", [D, 2, CROSS.width], F32R) for i in range(2)]
        K2b = [sb(f"K2_{i}", [STACK2, 2, CROSS.width], F32R) for i in range(2)]
        Q1b = [sb(f"Q1_{i}", [D, 2, 2, N], F32R) for i in range(2)]
        Q2b = [sb(f"Q2_{i}", [STACK2, 2, 2, N], F32R) for i in range(2)]
        Vb = [sb(f"V{i}", [D, len(CROSS.tiles), PAIR]) for i in range(2)]
        PR = [sb(f"P{i}", [D, 2, W]) for i in range(2)]
        psum_acc = sb("psum_acc", [D, 2, W])
        mx = sb("mx", [D, 4, len(CROSS.maxima)])
        nmx = sb("nmx", [D, 4])
        oraw = sb("oraw", [PAIR, N])
        inv = sb("inv", [PAIR, N])
        oT = sb("oT", [PAIR, N])

        S = [ctx.enter_context(nc.psum_tensor(f"S{i}", [D, 2, W], F32)) for i in range(2)]
        PB = [ctx.enter_context(nc.psum_tensor(f"PB{i}", [D, 512], F32)) for i in range(2)]
        TB = ctx.enter_context(nc.psum_tensor("TB", [D, 512], F32))
        OB = ctx.enter_context(nc.psum_tensor("OB", [D, 512], F32))

        def part(i, k):
            return Vb[i][:, 4 * k:4 * k + 4, :].rearrange("p a b -> p (a b)")

        xc, sq, sd = ([part(i, k) for i in range(2)] for k in range(3))
        xh = [krot[:, 0:512], krot[:, 512:1024]]
        w1_sb, w2_sb = PR[0][:, 0, 0:FF * D], PR[1][:, 0, 0:FF * D]

        s_const = sem("constants_loaded")
        s_ctx = sem("context_loaded")
        s_set = sem("constants_set")
        s_rows = sem("stack_rows_set")
        s_ada_mm = sem("adaln_products")
        s_mod = sem("adaln_vectors")
        s_bias = sem("biases_added")
        s_out = sem("output_stored")
        s_w1 = sem("ff_weights_loaded")
        s_h = sem("ff_hidden")
        s_g = sem("ff_gelu")
        s_f = sem("ff_out")
        s_y = sem("ff_added")

        class LayerNorm:

            def __init__(self, name):
                self.mean = sem(name + "_mean")
                self.centred = sem(name + "_centred")
                self.squared = sem(name + "_squared")
                self.var = sem(name + "_var")
                self.std = sem(name + "_std")
                self.inv = sem(name + "_inverse")
                self.unit = sem(name + "_unit")
                self.done = sem(name + "_done")

        class Steps:

            def __init__(self, a):
                n = a.name
                self.src = sem(n + "_source_loaded")
                self.w = [sem(f"{n}_weights_loaded{i}") for i in range(2)]
                self.wo = [sem(f"{n}_wo_loaded{i}") for i in range(UNROLL)]
                self.proj = sem(n + "_projected")
                self.maxp = sem(n + "_max_scores")
                self.freed = sem(n + "_projection_turned")
                self.rot = sem(n + "_rotated")
                self.vread = sem(n + "_v_read")
                self.qh = sem(n + "_q_high")
                self.ql = sem(n + "_q_low")
                self.kh = sem(n + "_k_high")
                self.k2 = sem(n + "_k_high2")
                self.kl = sem(n + "_k_low")
                self.mxr = sem(n + "_max_reduced")
                self.mx = sem(n + "_max")
                self.mt = sem(n + "_max_row")
                self.mrow = sem(n + "_max_row_copied")
                self.s = sem(n + "_scores")
                self.e = sem(n + "_exp")
                self.pv = sem(n + "_pv")
                self.acc = sem(n + "_acc")
                self.fold = sem(n + "_fold")
                self.oev = sem(n + "_o_read")
                self.sum = sem(n + "_sum")
                self.inv = sem(n + "_sum_inverse")
                self.ot = sem(n + "_o_scaled")
                self.y = sem(n + "_y")
                self.added = sem(n + "_added")

        LN1, LNX, LN2, LN3 = LayerNorm("ln1"), LayerNorm("lnx"), LayerNorm("ln2"), LayerNorm("ln3")
        sems = {"sa": Steps(SELF), "ca": Steps(CROSS)}

        def run_steps(eng, a, body):
            for j in range(-a.lead, UNROLL):
                body((0, j))
            with eng.Fori(1, STEPS // UNROLL - 1) as i:
                for r in range(UNROLL):
                    body((i, r))
            for r in range(UNROLL + 1):
                body((STEPS // UNROLL - 1, r))

        def later(j, by):
            return (j[0], j[1] + by)

        def exists(j):
            return not isinstance(j[0], int) or 0 <= UNROLL * j[0] + j[1] < STEPS

        def times(j, n):
            return j[0] * (UNROLL * n) + j[1] * n

        def batch(j):
            return (j[0] + j[1] // UNROLL) >> 1

        def wait(eng, semaphore, value):
            if not isinstance(value, int) or value > 0:
                eng.wait_ge(semaphore, value)

        def of_step(a, what, j):
            by = 0 if what in ("S", "E", "P", "oev") else -1 if what in ("sum", "div", "out", "add") else \
                1 if what in ("a", "mx", "M", "row") else a.lead
            return later(j, by)

        def slot(a, J):
            return J[1] % 2, J[1] % a.ring // 2

        def K1(a, J, rows, h, lo, hi):
            i, k = slot(a, J)
            return K1b[i][rows, h, k * N + lo:k * N + hi]

        def K2(a, J, rows, h, lo, hi):
            i, k = slot(a, J)
            return K2b[i][rows, h, k * N + lo:k * N + hi]

        def V(a, J, t):
            i, k = slot(a, J)
            return Vb[i][:, 2 * k + t, :]

        def Q1(a, J):
            i, k = slot(a, J)
            return Q1b[i][:, k]

        def Q2(a, J):
            i, k = slot(a, J)
            return Q2b[i][:, k]

        def half(h):
            return slice(h * DH, (h + 1) * DH)

        def group(a, g):
            first, last = a.project[a.groups[g][0]], a.project[a.groups[g][-1]]
            return first[0], last[0] + last[1]

        def run_chunks(eng, count, first, body):
            first()
            body(0, 0, True)
            body(1, 1, True)
            if count > 4:
                with eng.Fori(1, count // 2 - 1) as i:
                    body(2 * i, 0, True)
                    body(2 * i + 1, 1, True)
            body(count - 2, 0, True)
            body(count - 1, 1, False)

        block = ctx.enter_context(nc.Block())

        @block.sync
        def _(sp):
            for dst, source in ((cols, cols_in), (condT, cT_in), (ada, ada_in), (xT, xT_in),
                                (ropeq, rope_in[:, 2 * M:]), (ident, ident_in)):
                sp.dma_start(dst[:], source).then_inc(s_const, 16)

            def weights(a, s, J, pair):
                kv, wq, wo = packs[a.name]
                b, r = J[1] % 2, J[1] % UNROLL
                n = len(a.count["proj"])
                wait(sp, s.proj, times(J, n) - n)
                sp.dma_start(kv_w[b][0:a.rows, :], kv[pair]).then_inc(s.w[b], 16)
                sp.dma_start(q_w[b][:, :], wq[pair]).then_inc(s.w[b], 16)
                wait(sp, s.y, times(J, 1) - UNROLL + 1)
                sp.dma_start(o_w[r][:, :], wo[pair]).then_inc(s.wo[r], 16)

            def source(a, s, b):
                wait(sp, s.proj, b * (PAIRS * len(a.count["proj"])))
                keys = ainT if a is SELF else ctxT_all
                sp.dma_start(qsrc[:, :], ainT[:, bass.ds(b * N, N)]).then_inc(s.src, 16)
                sp.dma_start(src[0:a.rows, 0:a.keys], keys[0:a.rows, bass.ds(b * a.keys, a.keys)]
                             ).then_inc(s.src, 16)

            for a, ln in ((SELF, LN1), (CROSS, LN2)):
                s = sems[a.name]
                if a is CROSS:
                    sp.wait_ge(LNX.done, NCL)
                sp.wait_ge(ln.done, 2 * NLN)
                source(a, s, 0)
                for r in range(PAIRS):
                    weights(a, s, (0, r), r)
                    if a is SELF and r == 1:
                        sp.dma_start(cols96[:], cols96_in).then_inc(s_ctx, 16)
                        sp.wait_ge(s_set, 5)
                        sp.dma_start(ctxT_all[:, 0:B * M], ctxT_in).then_inc(s_ctx, 16)
                        sp.dma_start(rope[:], rope_in[:, 0:2 * M]).then_inc(s_ctx, 16)
                with sp.Fori(1, B) as b:
                    source(a, s, b)
                    for r in range(PAIRS):
                        weights(a, s, (b * 2, r), r)
            s = sems["ca"]
            sp.wait_ge(s.pv, len(CROSS.chunks) * STEPS)
            sp.wait_ge(s.acc, len(CROSS.chunks) * STEPS)
            sp.dma_start(w1_sb, w1_in).then_inc(s_w1, 16)
            sp.dma_start(w2_sb, w2_in).then_inc(s_w1, 16)
            for c in range(NLN):
                sp.wait_ge(s_y, c + 1)
                sp.dma_start(outT[:, c * LNC:(c + 1) * LNC], xT[:, c * LNC:(c + 1) * LNC]
                             ).then_inc(s_out, 16)
            sp.wait_ge(s_out, 16 * NLN)

        @block.gpsimd
        def _(pool):
            pool.memset(meanw[:], 1.0 / D).then_inc(s_set, 1)
            pool.memset(meanw96[:], 1.0 / DC).then_inc(s_set, 1)
            pool.memset(onesw[:], 1.0).then_inc(s_set, 1)
            pool.memset(epsc[:], EPS).then_inc(s_set, 1)
            pool.memset(ctxT_all[:, B * M:NCL * CLN], 0.0).then_inc(s_set, 1)

            a, s = CROSS, sems["ca"]
            n, rows, last = len(a.chunks), a.tile, a.tiles[-1][1]

            def body(j):
                if not exists(j):
                    return
                for c in range(1, n):
                    P = PR[(j[1] * n + c) % 2]
                    wait(pool, s.e, times(j, n) + c + 1)
                    if c == 1:
                        wait(pool, s.sum, times(j, 1))
                        pool.tensor_tensor(psum_acc[0:rows], PR[(j[1] * n) % 2][0:rows], P[0:rows], ALU.add
                                           ).then_inc(s.acc, 2)
                    elif c < n - 1:
                        wait(pool, s.acc, times(j, n) + c)
                        pool.tensor_tensor(psum_acc[0:rows], psum_acc[0:rows], P[0:rows], ALU.add
                                           ).then_inc(s.acc, 1)
                    else:
                        wait(pool, s.fold, times(j, 1) + 1)
                        pool.tensor_tensor(psum_acc[0:last, 0], psum_acc[0:last, 0], P[0:last, 0], ALU.add
                                           ).then_inc(s.acc, 1)
                    if c == n - 2:
                        wait(pool, s.acc, times(j, n) + c + 1)
                        pool.tensor_tensor(psum_acc[0:rows, 0], psum_acc[0:rows, 0], psum_acc[0:rows, 1],
                                           ALU.add).then_inc(s.fold, 1)

            run_steps(pool, a, body)

        @block.scalar
        def _(act):
            def copy(out, in_):
                return act.activation(out, in_, ACT.Copy)

            def norm(ln, count, rows, width):
                def square(c, r):
                    wait(act, ln.centred, c + 1)
                    wait(act, ln.var, c - 1)
                    act.activation(sq[r][0:rows, 0:width], xc[r][0:rows, 0:width], ACT.Square
                                   ).then_inc(ln.squared, 1)

                def body(c, r, more):
                    if more:
                        square(c + 1, 1 - r)
                    wait(act, ln.var, c + 1)
                    wait(act, ln.unit, c - 1)
                    act.activation(sd[r][0:rows, 0:width], S[r][0:rows, 1, 0:width], ACT.Sqrt,
                                   bias=epsc[0:rows, :]).then_inc(ln.std, 1)

                run_chunks(act, count, lambda: square(0, 0), body)

            def attention(a, s):
                n, nk, ng, nv = len(a.chunks), len(a.project), len(a.groups), len(a.vgroups)
                np_ = len(a.count["proj"])

                def exponentials(j, c):
                    rows, k, i = a.tiles[a.chunks[c][0]][1], len(a.chunks[c]), (j[1] * n + c) % 2
                    wait(act, s.s, times(j, n) + c + 1)
                    wait(act, s.pv, times(j, n) + c - 1)
                    if a is CROSS:
                        wait(act, s.acc, times(j, n) + c - 1)
                    else:
                        wait(act, s.sum, times(j, 1) - 1)
                    act.activation(PR[i][0:rows, 0:k], S[i][0:rows, 0:k], ACT.Exp, scale=SCALE
                                   ).then_inc(s.e, 1)

                def q_high(J):
                    wait(act, s.rot, times(J, 1 + nk) + 1)
                    wait(act, s.s, times(J, n) - n * (a.ring - 1))
                    for h in range(2):
                        for k in range(2):
                            ins = copy(Q1(a, J)[half(k), h, :], qrot[half(h), :])
                    ins.then_inc(s.qh, 1)

                def k_high(J, g):
                    lo, hi = group(a, g)
                    wait(act, s.rot, times(J, 1 + nk) + 2 + a.groups[g][-1])
                    wait(act, s.s, times(J, n) - n * (a.ring - 1))
                    for h in range(2):
                        ins = copy(K1(a, J, half(h), h, lo, hi), krot[half(h), lo:hi])
                    ins.then_inc(s.kh, 1)
                    for h in range(2):
                        ins = copy(K2(a, J, half(0), h, lo, hi), krot[half(h), lo:hi])
                    ins.then_inc(s.k2, 1)

                def v_out(J, v):
                    wait(act, s.proj, times(J, np_) + a.count["proj"].index(("v", v)) + 1)
                    wait(act, s.pv, times(J, n) - n * (a.ring - 1))
                    bank = PB[a.bank[("v", v)]]
                    ts = a.vgroups[v]
                    full = [t for t in ts if a.tiles[t][1] == a.tile]
                    i, k = slot(a, J)
                    if full:
                        ins = copy(Vb[i][0:a.tile, 2 * k + full[0]:2 * k + full[-1] + 1, :],
                                   bank[0:a.tile, 0:len(full) * PAIR].rearrange("p (t n) -> p t n", n=PAIR))
                    for t in ts:
                        if t not in full:
                            w = a.tiles[t][1]
                            at = (t - ts[0]) * PAIR
                            ins = copy(V(a, J, t)[0:w], bank[0:w, at:at + PAIR])
                    ins.then_inc(s.vread, 1)

                def body(j):
                    for what, k in a.act:
                        J = of_step(a, what, j)
                        if not exists(J):
                            continue
                        if what == "E":
                            exponentials(J, k)
                        if what == "q":
                            q_high(J)
                        if what == "g":
                            k_high(J, k)
                        if what == "v":
                            v_out(J, k)

                run_steps(act, a, body)

            act.wait_ge(s_set, 4)
            norm(LN1, NLN, D, LNC)
            attention(SELF, sems["sa"])
            norm(LN2, NLN, D, LNC)
            norm(LNX, NCL, DC, CLN)
            attention(CROSS, sems["ca"])
            norm(LN3, NLN, D, LNC)
            for n in range(NLN * FF):
                f = n % FF
                act.wait_ge(s_h, n + 1)
                wait(act, s_f, n - 1)
                act.activation(turned[n % 2][:, :], PB[n % 2][:, :], ACT.Gelu, bias=cols[:, 12 + f:13 + f]
                               ).then_inc(s_g, 1)

        @block.vector
        def _(dve):
            def adaln_vectors():
                dve.wait_ge(s_ada_mm, 1)
                n = 0
                for i in range(2):
                    dve.tensor_scalar(modt[:, 2 * i, :], OB[:, 16 * i:16 * i + B], cols[:, 4 * i + 2:4 * i + 3],
                                      1.0, ALU.add, ALU.add).then_inc(s_mod, 1)
                    dve.tensor_scalar(modt[:, 2 * i + 1, :], OB[:, 16 * i + 8:16 * i + 8 + B],
                                      cols[:, 4 * i + 3:4 * i + 4], None, ALU.add).then_inc(s_mod, 1)
                    n += 2
                    dve.wait_ge(s_mod, n)
                    dve.tensor_scalar(mod[:, 2 * i, :], modt[:, 2 * i, :], cols[:, 4 * i:4 * i + 1], None,
                                      ALU.mult).then_inc(s_mod, 1)
                    dve.scalar_tensor_tensor(out=mod[:, 2 * i + 1, :], in0=modt[:, 2 * i, :],
                                             scalar=cols[:, 4 * i + 1:4 * i + 2], in1=modt[:, 2 * i + 1, :],
                                             op0=ALU.mult, op1=ALU.add).then_inc(s_mod, 1)
                    n += 2
                dve.wait_ge(s_mod, n)

            def norm(ln, count, rows, width, x, output):
                def centre(c, r):
                    wait(dve, ln.mean, c + 1)
                    wait(dve, ln.squared, c - 1)
                    wait(dve, ln.unit, c - 1)
                    dve.tensor_tensor(xc[r][0:rows, 0:width], x(c), S[r][0:rows, 0, 0:width], ALU.subtract
                                      ).then_inc(ln.centred, 1)

                def body(c, r, more):
                    if more:
                        centre(c + 1, 1 - r)
                    wait(dve, ln.std, c + 1)
                    dve.reciprocal(xh[r][0:rows, 0:width], sd[r][0:rows, 0:width]).then_inc(ln.inv, 1)
                    wait(dve, ln.inv, c + 1)
                    dve.tensor_tensor(xh[r][0:rows, 0:width], xh[r][0:rows, 0:width],
                                      xc[r][0:rows, 0:width], ALU.mult).then_inc(ln.unit, 1)
                    wait(dve, ln.unit, c + 1)
                    output(c, xh[r][0:rows, 0:width])

                run_chunks(dve, count, lambda: centre(0, 0), body)

            def adaln(ln, i):
                def output(c, unit):
                    for h in range(2):
                        b = 2 * c + h
                        dve.tensor_scalar(ainT[:, b * N:(b + 1) * N], unit[:, h * N:(h + 1) * N],
                                          mod[:, 2 * i, b:b + 1], mod[:, 2 * i + 1, b:b + 1],
                                          ALU.mult, ALU.add).then_inc(ln.done, 1)

                norm(ln, NLN, D, LNC, lambda c: xT[:, c * LNC:(c + 1) * LNC], output)

            def add_bias(k, n):
                dve.tensor_scalar(xT[:, :], xT[:, :], cols[:, k:k + 1], None, ALU.add).then_inc(s_bias, 1)
                dve.wait_ge(s_bias, n)

            def attention(a, s):
                n, nk, ng, nm = len(a.chunks), len(a.project), len(a.groups), len(a.maxima)
                np_, na = len(a.count["proj"]), len(a.count["a"])
                table = ropeq if a is SELF else rope

                def rotate(J, w, m, tab, out, cols_):
                    i = m % 2
                    wait(dve, s.proj, times(J, np_) + a.count["proj"].index(w) + 1)
                    wait(dve, s.rot, times(J, 1 + nk) + m - 1)
                    dve.tensor_tensor(turned[i][:, 0:2 * cols_], PB[a.bank[w]][:, 0:2 * cols_], tab, ALU.mult
                                      ).then_inc(s.freed, 1)
                    wait(dve, s.freed, times(J, 1 + nk) + m + 1)
                    if m == 0:
                        wait(dve, s.qh, times(J, 1))
                        wait(dve, s.ql, times(J, 1))
                    if m == 1:
                        wait(dve, s.k2, times(J, ng))
                        wait(dve, s.kl, times(J, ng))
                    dve.tensor_tensor(out, turned[i][:, 0:cols_], turned[i][:, cols_:2 * cols_], ALU.add
                                      ).then_inc(s.rot, 1)

                def q_low(J):
                    wait(dve, s.qh, times(J, 1) + 1)
                    for h in range(2):
                        ins = dve.tensor_tensor(Q2(a, J)[0:DH, h, :], qrot[half(h), :],
                                                Q1(a, J)[half(h), h, :].bitcast(F32), ALU.subtract)
                    ins.then_inc(s.ql, 1)

                def k_low(J, g):
                    lo, hi = group(a, g)
                    wait(dve, s.kh, times(J, ng) + g + 1)
                    for h in range(2):
                        ins = dve.tensor_tensor(K1(a, J, half(1 - h), h, lo, hi), krot[half(h), lo:hi],
                                                K1(a, J, half(h), h, lo, hi).bitcast(F32), ALU.subtract)
                    ins.then_inc(s.kl, 1)

                def maximum(J, k):
                    bank = PB[a.bank[("a", k)]]
                    wait(dve, s.maxp, times(J, na) + k + 1)
                    if a is SELF:
                        wait(dve, s.mt, times(J, 1))
                        dve.tensor_reduce(nmx[:, 2 * k:2 * k + 2], bank[:, :].rearrange("p (t n) -> p t n", n=N),
                                          AX.X, ALU.max, negate=True).then_inc(s.mxr, 1)
                    else:
                        c, hq = k // 4, k % 4
                        if k == 0:
                            wait(dve, s.mx, times(J, 1))
                        dve.tensor_reduce(mx[:, hq, c:c + 1], bank[:, 0:a.maxima[c][1]], AX.X, ALU.max
                                          ).then_inc(s.mxr, 1)

                def last_maximum(J):
                    wait(dve, s.mxr, times(J, na) + na)
                    wait(dve, s.mt, times(J, 1))
                    dve.tensor_reduce(nmx[:, :], mx[:, :, 0:nm], AX.X, ALU.max, negate=True
                                      ).then_inc(s.mx, 1)

                def max_row(J):
                    wait(dve, s.mt, times(J, 1) + 1)
                    dve.tensor_copy(Q2(a, J)[DH:DH + 1].rearrange("p h n -> p (h n)"), TB[DH:DH + 1, :]
                                    ).then_inc(s.mrow, 1)

                def o_out(j):
                    wait(dve, s.pv, times(j, n) + n)
                    wait(dve, s.ot, times(j, 1))
                    dve.tensor_copy(oraw[:, :], OB[:, 0:N]).then_inc(s.oev, 1)

                def divide(j):
                    wait(dve, s.sum, times(j, 1) + 1)
                    wait(dve, s.ot, times(j, 1))
                    dve.reciprocal(inv[:, :], TB[:, 0:N]).then_inc(s.inv, 1)
                    wait(dve, s.inv, times(j, 1) + 1)
                    wait(dve, s.oev, times(j, 1) + 1)
                    wait(dve, s.y, times(j, 1))
                    dve.tensor_tensor(oT[:, :], oraw[:, :], inv[:, :], ALU.mult).then_inc(s.ot, 1)

                def add(j):
                    wait(dve, s.y, times(j, 1) + 1)
                    wait(dve, s.added, times(j, 1))
                    b = nc.s_assert_within(batch(j), 0, B - 1, skip_runtime_bounds_check_because=
                                           "there are PAIRS steps for each of the B batches")
                    dve.tensor_tensor(xT[:, bass.ds(b * N, N)], xT[:, bass.ds(b * N, N)], TB[:, 0:N],
                                      ALU.add).then_inc(s.added, 1)

                def body(j):
                    for what, k in a.dve:
                        J = of_step(a, what, j)
                        if not exists(J):
                            continue
                        if what == "q":
                            rotate(J, (what, k), 0, ropeq[:, :], qrot[:, :], N)
                        if what == "k":
                            lo, w = a.project[k]
                            rotate(J, (what, k), 1 + k, table[:, 2 * lo:2 * (lo + w)], krot[:, lo:lo + w], w)
                        if what == "ql":
                            q_low(J)
                        if what == "l":
                            k_low(J, k)
                        if what == "a":
                            maximum(J, k)
                        if what == "mx":
                            last_maximum(J)
                        if what == "row":
                            max_row(J)
                        if what == "oev":
                            o_out(J)
                        if what == "div":
                            divide(J)
                        if what == "add":
                            add(J)

                run_steps(dve, a, body)
                dve.wait_ge(s.added, STEPS)

            for i in range(2):
                dve.memset(K2b[i][DH:STACK2].bitcast(F32), 0.0).then_inc(s_rows, 1)
                dve.memset(Q2b[i][DH:STACK2].bitcast(F32), 0.0).then_inc(s_rows, 1)
                dve.memset(K1b[i][:, :, CROSS.keys:CROSS.width].bitcast(F32), 0.0).then_inc(s_rows, 1)
            dve.wait_ge(s_rows, 6)
            for i in range(2):
                dve.memset(K2b[i][DH:DH + 1].bitcast(F32), 1.0).then_inc(s_rows, 1)
            dve.wait_ge(s_rows, 8)
            dve.wait_ge(s_const, 16 * 6)
            adaln_vectors()
            adaln(LN1, 0)
            add_bias(8, 1)
            attention(SELF, sems["sa"])
            adaln(LN2, 0)
            add_bias(9, 2)
            dve.wait_ge(s_ctx, 48)

            def context(c):
                return ctxT_all[:, bass.ds(c * CLN, CLN)]

            def context_out(c, unit):
                dve.tensor_scalar(context(c), unit, cols96[:, 0:1], cols96[:, 1:2], ALU.mult, ALU.add
                                  ).then_inc(LNX.done, 1)

            norm(LNX, NCL, DC, CLN, context, context_out)
            attention(CROSS, sems["ca"])
            adaln(LN3, 1)
            add_bias(10, 3)
            for c in range(NLN):
                dve.wait_ge(s_f, (c + 1) * FF)
                dve.tensor_tensor(xT[:, c * LNC:(c + 1) * LNC], xT[:, c * LNC:(c + 1) * LNC],
                                  (OB, TB)[c % 2][:, :], ALU.add).then_inc(s_y, 1)

        @block.tensor
        def _(pe):
            def norm(ln, count, rows, width, x, weights):
                def mean(c, r):
                    wait(pe, ln.centred, c - 1)
                    pe.matmul(S[r][0:rows, 0, 0:width], weights, x(c), start=True, stop=True
                              ).then_inc(ln.mean, 1)

                def body(c, r, more):
                    if more:
                        mean(c + 1, 1 - r)
                    wait(pe, ln.squared, c + 1)
                    wait(pe, ln.std, c - 1)
                    pe.matmul(S[r][0:rows, 1, 0:width], weights, sq[r][0:rows, 0:width], start=True, stop=True
                              ).then_inc(ln.var, 1)

                run_chunks(pe, count, lambda: mean(0, 0), body)

            def norm_x(ln):
                norm(ln, NLN, D, LNC, lambda c: xT[:, c * LNC:(c + 1) * LNC], meanw[:, :])

            def attention(a, s):
                n, nk, ng, nv, nm = (len(a.chunks), len(a.project), len(a.groups), len(a.vgroups),
                                     len(a.maxima))
                na = len(a.count["a"])

                def bank(J, w):
                    last, back = a.before[w]
                    k = later(J, -back)
                    if last[0] == "v":
                        wait(pe, s.vread, times(k, nv) + last[1] + 1)
                    elif last[0] == "a":
                        wait(pe, s.mxr, times(k, na) + last[1] + 1)
                    else:
                        wait(pe, s.freed, times(k, 1 + nk) + a.count["qk"].index(last) + 1)
                    return PB[a.bank[w]]

                def q_projection(J):
                    out = bank(J, ("q", 0))
                    b = J[1] % 2
                    wait(pe, s.w[b], (J[0] * 2 + J[1] // 2) * 32 + 32)
                    wait(pe, s.src, batch(J) * 32 + 32)
                    for i in range(2):
                        ins = pe.matmul(out[:, i * N:(i + 1) * N], q_w[b][:, i * PAIR:(i + 1) * PAIR],
                                        qsrc[:, :], start=True, stop=True)
                    ins.then_inc(s.proj, 1)

                def k_projection(J, k):
                    out = bank(J, ("k", k))
                    b = J[1] % 2
                    lo, w = a.project[k]
                    for i in range(2):
                        ins = pe.matmul(out[:, i * w:(i + 1) * w], kv_w[b][0:a.rows, i * PAIR:(i + 1) * PAIR],
                                        src[0:a.rows, lo:lo + w], start=True, stop=True)
                    ins.then_inc(s.proj, 1)

                def v_projection(J, v):
                    out = bank(J, ("v", v))
                    b = J[1] % 2
                    for k, t in enumerate(a.vgroups[v]):
                        lo, w = a.tiles[t]
                        ins = pe.matmul(out[0:w, k * PAIR:(k + 1) * PAIR], src[0:a.rows, lo:lo + w],
                                        kv_w[b][0:a.rows, 2 * PAIR:3 * PAIR], start=True, stop=True)
                    ins.then_inc(s.proj, 1)

                def max_scores(J, k):
                    out = bank(J, ("a", k))
                    if k == 0:
                        wait(pe, s.qh, times(J, 1) + 1)
                    if a is SELF:
                        wait(pe, s.kl, times(J, ng) + ng)
                        for qt in range(2):
                            ins = pe.matmul(out[:, qt * N:(qt + 1) * N], Q1(a, J)[:, k, qt * 128:(qt + 1) * 128],
                                            K1(a, J, slice(0, D), k, 0, N), start=True, stop=True)
                    else:
                        c, h, qt = k // 4, k % 4 // 2, k % 2
                        lo, w = a.maxima[c]
                        if h == qt == 0:
                            g = [i for i in range(ng) if group(a, i)[1] >= lo + w][0]
                            wait(pe, s.kl, times(J, ng) + g + 1)
                        w += w % 2
                        ins = pe.matmul(out[:, 0:w], Q1(a, J)[:, h, qt * 128:(qt + 1) * 128],
                                        K1(a, J, slice(0, D), h, lo, lo + w), start=True, stop=True)
                    ins.then_inc(s.maxp, 1)

                def max_row(J):
                    if a is SELF:
                        wait(pe, s.mxr, times(J, na) + na)
                        wait(pe, s.ot, times(J, 1) - 1)
                    else:
                        wait(pe, s.mx, times(J, 1) + 1)
                        wait(pe, s.added, times(J, 1) - 1)
                    for hq in range(4):
                        ins = pe.matmul(TB[DH:DH + 1, hq * 128:(hq + 1) * 128], nmx[:, hq:hq + 1],
                                        ident[:, :], start=True, stop=True)
                    ins.then_inc(s.mt, 1)

                def scores(j, c):
                    i = (j[1] * n + c) % 2
                    if c == 0:
                        wait(pe, s.k2, times(j, ng) + ng)
                        wait(pe, s.kl, times(j, ng) + ng)
                        wait(pe, s.ql, times(j, 1) + 1)
                        wait(pe, s.mrow, times(j, 1) + 1)
                    wait(pe, s.e, times(j, n) + c - 1)
                    for k, t in enumerate(a.chunks[c]):
                        lo, w = a.tiles[t]
                        for h in range(2):
                            out = S[i][0:w, k, h * N:(h + 1) * N]
                            pe.matmul(out, K1(a, j, slice(0, D), h, lo, lo + w), Q1(a, j)[:, h, :],
                                      start=True, stop=False)
                            ins = pe.matmul(out, K2(a, j, slice(0, STACK2), h, lo, lo + w), Q2(a, j)[:, h, :],
                                            start=False, stop=True)
                    ins.then_inc(s.s, 1)

                def products(j, c):
                    i = (j[1] * n + c) % 2
                    if c == 0:
                        wait(pe, s.vread, times(j, nv) + nv)
                        wait(pe, s.oev, times(j, 1))
                    wait(pe, s.e, times(j, n) + c + 1)
                    for k, t in enumerate(a.chunks[c]):
                        w = a.tiles[t][1]
                        for h in range(2):
                            ins = pe.matmul(OB[half(h), 0:N], V(a, j, t)[0:w, half(h)],
                                            PR[i][0:w, k, h * N:(h + 1) * N], start=(t == 0),
                                            stop=(t == len(a.tiles) - 1))
                    ins.then_inc(s.pv, 1)

                def sums(j):
                    wait(pe, s.added, times(j, 1))
                    if exists(later(j, 1)):
                        wait(pe, s.mrow, times(j, 1) + 2)
                    if a is SELF:
                        parts = (PR[j[1] % 2][:, 0], PR[j[1] % 2][:, 1])
                    else:
                        wait(pe, s.acc, times(j, n) + n)
                        parts = (psum_acc[0:a.tile, 0],)
                    for h in range(2):
                        for k, p in enumerate(parts):
                            ins = pe.matmul(TB[half(h), 0:N], onesw[0:a.tile, :], p[:, h * N:(h + 1) * N],
                                            start=(k == 0), stop=(k == len(parts) - 1))
                    ins.then_inc(s.sum, 1)

                def output(j):
                    r = j[1] % UNROLL
                    wait(pe, s.wo[r], (j[0] + j[1] // UNROLL) * 16 + 16)
                    wait(pe, s.ot, times(j, 1) + 1)
                    if a is SELF and exists(later(j, 2)):
                        wait(pe, s.mrow, times(j, 1) + 3)
                    pe.matmul(TB[:, 0:N], o_w[r][:, :], oT[:, :], start=True, stop=True).then_inc(s.y, 1)

                def body(j):
                    for what, k in a.pe:
                        J = of_step(a, what, j)
                        if not exists(J):
                            continue
                        if what == "S":
                            scores(J, k)
                        if what == "P":
                            products(J, k)
                        if what == "q":
                            q_projection(J)
                        if what == "k":
                            k_projection(J, k)
                        if what == "v":
                            v_projection(J, k)
                        if what == "a":
                            max_scores(J, k)
                        if what == "M":
                            max_row(J)
                        if what == "sum":
                            sums(J)
                        if what == "out":
                            output(J)

                run_steps(pe, a, body)
                pe.wait_ge(s.added, STEPS)

            pe.wait_ge(s_const, 16 * 6)
            pe.wait_ge(s_set, 4)
            for i in range(4):
                ins = pe.matmul(OB[:, 8 * i:8 * i + B], ada[:, i * D:(i + 1) * D], condT[:, :], start=True,
                                stop=True)
            ins.then_inc(s_ada_mm, 1)
            norm_x(LN1)
            attention(SELF, sems["sa"])
            norm_x(LN2)
            pe.wait_ge(s_ctx, 48)
            norm(LNX, NCL, DC, CLN, lambda c: ctxT_all[:, bass.ds(c * CLN, CLN)], meanw96[:, :])
            attention(CROSS, sems["ca"])
            norm_x(LN3)
            pe.wait_ge(s_w1, 32)

            def hidden(n):
                c, f = n // FF, n % FF
                pe.wait_ge(LN3.done, 2 * (c + 1))
                wait(pe, s_g, n - 1)
                pe.matmul(PB[n % 2][:, :], w1_sb[:, f * D:(f + 1) * D], ainT[:, c * LNC:(c + 1) * LNC],
                          start=True, stop=True).then_inc(s_h, 1)

            hidden(0)
            for n in range(NLN * FF):
                c, f = n // FF, n % FF
                if n + 1 < NLN * FF:
                    hidden(n + 1)
                pe.wait_ge(s_g, n + 1)
                if f == 0:
                    wait(pe, s_y, c - 1)
                pe.matmul((OB, TB)[c % 2][:, :], w2_sb[:, f * D:(f + 1) * D], turned[n % 2][:, :],
                          start=(f == 0), stop=(f == FF - 1)).then_inc(s_f, 1)


def kernel(**inputs):
    import concourse.bacc as bacc
    from concourse.bass_utils import run_bass_kernel_spmd

    a = {k.removeprefix("L0_xcond_"): np.asarray(v) for k, v in inputs.items()}
    B, n, D_ = a["x"].shape
    M = a["ctx_768"].shape[1]
    pairs = a["sa_wq"].shape[1] // PAIR

    def halves(w, swap):
        w = w.reshape(w.shape[0], pairs, 2, DH // 2, 2)
        w = w[..., ::-1] if swap else w
        return w.transpose(1, 0, 2, 4, 3).reshape(pairs, w.shape[0], PAIR)

    def packs(p):
        wk, wv = np.split(a[p + "_wkv"], 2, axis=1)
        wv = wv.reshape(wv.shape[0], pairs, PAIR).transpose(1, 0, 2)
        kv = np.concatenate([halves(wk, False), halves(wk, True), wv], axis=2)
        wq = a[p + "_wq"]
        return kv, np.concatenate([halves(wq, False), halves(wq, True)], axis=2), \
            a[p + "_wo"].reshape(pairs, PAIR, D_)

    inv = np.float32(1) / (10000.0 ** (np.arange(0, DH, 2) / DH)).astype(np.float32)
    ang = np.arange(M, dtype=np.float32)[:, None] * inv[None, :]
    cos, sin = np.cos(ang).T, np.sin(ang).T
    C = np.concatenate([cos] * 4, 0)
    Sg = np.concatenate([-sin, sin] * 2, 0)

    def interleave(keys, chunk):
        out = []
        for lo in range(0, keys, chunk):
            hi = min(lo + chunk, keys)
            out += [C[:, lo:hi], Sg[:, lo:hi]]
        return out

    rope = np.concatenate(interleave(M, 229) + interleave(n, n), axis=1)
    ff = a["ff_w1"].shape[1] // D_
    cols = np.stack([a["ln1_w"], a["ln1_b"], a["g1_b"], a["b1_b"], a["ln2_w"], a["ln2_b"], a["g2_b"],
                     a["b2_b"], a["sa_bo"], a["ca_bo"], a["ff_b2"], a["ff_b2"]]
                    + list(a["ff_b1"].reshape(ff, D_)), axis=1)
    arrays = {
        "xT": a["x"].transpose(2, 0, 1).reshape(D_, B * n),
        "condT": a["cond_1024"].T,
        "ctxT": a["ctx_768"].transpose(2, 0, 1).reshape(-1, B * M),
        "cols": cols,
        "cols96": np.stack([a["ca_lnc_w"], a["ca_lnc_b"]], axis=1),
        "ada": np.concatenate([a["g1_w"], a["b1_w"], a["g2_w"], a["b2_w"]], axis=1),
        "w1": a["ff_w1"],
        "w2": a["ff_w2"].reshape(ff, D_, D_).transpose(1, 0, 2).reshape(D_, ff * D_),
        "rope": rope,
        "ident": np.eye(D_, dtype=np.float32),
    }
    for p in ("sa", "ca"):
        for name, w in zip(("kv", "wq", "wo"), packs(p)):
            arrays[f"{p}_{name}"] = w
    arrays = {k: np.ascontiguousarray(v) for k, v in arrays.items()}

    nc = bacc.Bacc("TRN2", target_bir_lowering=False, num_devices=1)
    t = {k: nc.dram_tensor(k + "_dram", v.shape, F32, kind="ExternalInput").ap() for k, v in arrays.items()}
    out = nc.dram_tensor("outT_dram", (D_, B * n), F32, kind="ExternalOutput").ap()
    block_kernel(nc, t["xT"], t["condT"], t["ctxT"], t["cols"], t["cols96"], t["ada"],
                 {p: (t[p + "_kv"], t[p + "_wq"], t[p + "_wo"]) for p in ("sa", "ca")},
                 t["w1"], t["w2"], t["rope"], t["ident"], out)
    r = run_bass_kernel_spmd(nc, [{k + "_dram": v for k, v in arrays.items()}], core_ids=[0])
    return r.results[0]["outT_dram"].reshape(D_, B, n).transpose(1, 2, 0)
```

```python
from contextlib import ExitStack

import concourse.bass as bass
import numpy as np
from concourse import mybir

F32 = mybir.dt.float32
F32R = mybir.dt.float32r
ALU = mybir.AluOpType
ACT = mybir.ActivationFunctionType
AX = mybir.AxisListType

D = 128
DH = 64
PAIR = 2 * DH
N = 256
W = 2 * N
EPS = 1e-5
SCALE = DH ** -0.5
UNROLL = 4
GROUP = 4
BANKS = 3
SLOTS = 4
STACK2 = 96


class Attention:

    def __init__(self, name, keys, rows, tile, project, maximum, lead, pe, dve, act, pool):
        self.name, self.keys, self.rows, self.tile, self.lead = name, keys, rows, tile, lead
        self.pe, self.dve, self.act, self.pool = ([(w.rstrip("0123456789"), int("0" + w.lstrip("abcdefghijklmnopqrstuvwxyzSEPM")))
                                        for w in text.split()] for text in (pe, dve, act, pool))
        self.tiles = [(a, min(tile, keys - a)) for a in range(0, keys, tile)]
        self.chunks = [list(range(a, min(a + 2, len(self.tiles)))) for a in range(0, len(self.tiles), 2)]
        self.project = [(a, min(project, keys - a)) for a in range(0, keys, project)]
        self.vgroups = [list(range(a, min(a + 4, len(self.tiles)))) for a in range(0, len(self.tiles), 4)]
        self.maxima = [(a, maximum) for a in range(0, keys - maximum + 1, maximum)]
        self.maxima[-1] = (self.maxima[-1][0], keys - self.maxima[-1][0])
        self.width = keys + keys % 2
        self.ring = 2 * lead
        self.kept = lead
        self.rotations = 1 + len(self.project)
        uses = [w for w in self.pe if w[0] in ("q", "k", "v", "a", "M", "sum", "out")]
        self.bank = {w: i % BANKS for i, w in enumerate(uses)}
        self.before = {}
        for w in uses:
            same = [v for v in uses if self.bank[v] == self.bank[w]]
            last = same[same.index(w) - 1]
            ahead = {v: {"a": 1, "M": 1, "sum": -1, "out": -1}.get(v[0], lead) for v in (w, last)}
            self.before[w] = (last, int(w == same[0]) + ahead[w] - ahead[last])
        self.count = {"proj": [w for w in uses if w[0] in ("q", "k", "v")], "a": [w for w in uses if w[0] == "a"],
                      "v": [w for w in uses if w[0] == "v"], "qk": [w for w in uses if w[0] in ("q", "k")]}


def block_kernel(nc, xT_in, cT_in, ctxT_in, cols_in, cols96_in, ada_in, packs, w1_in, w2_in,
                 rope_in, ident_in, outT):
    T = xT_in.shape[1]
    B = T // N
    M = ctxT_in.shape[1] // B
    DC = ctxT_in.shape[0]
    PAIRS = packs["sa"][0].shape[0]
    STEPS = B * PAIRS
    FF = w1_in.shape[1] // D
    LNC = 512
    NLN = T // LNC
    CLN = 402
    NCL = 32
    SELF = Attention("sa", N, D, 128, N, N, 2,
                      "q k0 sum S0 v0 a0 a1 P0 out M",
                      "q k0 div a0 a1 rq add r0",
                      "E0 v0 row oev g0 q",
                      "l0 ql")
    CROSS = Attention("ca", M, DC, 124, 401, 400, 1,
                      "q k0 k1 sum S0 S1 v0 k2 out k3 P0 S2 P1 a0 a1 v1 S3 a2 a3 P2 a4 a5 v2 S4 a6 a7 "
                      "a8 P3 a9 a10 S5 a11 P4 a12 a13 a14 a15 S6 P5 M v3 P6",
                      "q k0 k1 div rq k2 r0 add k3 l0 r1 a0 a1 r2 l1 a2 a3 a4 a5 l2 r3 a6 a7 a8 a9 l3 "
                      "a10 a11 a12 a13 a14 a15 mx ql",
                      "E0 E1 v0 q g0 E2 g1 v1 g2 E3 v2 E4 g3 E5 E6 v3 row oev",
                      "c1 c2 c3 c4 c5 c6")
    assert B == PAIRS == 2 * UNROLL and LNC == 2 * N and NCL * CLN >= B * M

    with ExitStack() as ctx:
        def sb(name, shape, dt=F32):
            return ctx.enter_context(nc.sbuf_tensor(name, shape, dt))

        def sem(name):
            return ctx.enter_context(nc.semaphore(name))

        xT = sb("xT", [D, T])
        ainT = sb("ainT", [D, T])
        ctxT_all = sb("ctxT_all", [DC, NCL * CLN])
        cols = sb("cols", [D, cols_in.shape[1]])
        cols96 = sb("cols96", [DC, 2])
        condT = sb("condT", [D, B])
        mod = sb("mod", [D, 4, B])
        epsc = sb("epsc", [D, 1])
        meanw = sb("meanw", [D, D])
        onesw = sb("onesw", [D, DH])
        ident = sb("ident", [D, D])
        rope = sb("rope", [PAIR, 2 * M])
        ropeq = sb("ropeq", [PAIR, 2 * N])

        kv_w = [sb(f"kv_w{i}", [D, 2 * PAIR]) for i in range(2)]
        q_w = [sb(f"q_w{i}", [D, PAIR]) for i in range(2)]
        o_w = [sb(f"o_w{i}", [PAIR, D]) for i in range(UNROLL)]
        src = sb("src", [D, M])
        select = src[:, 0:GROUP * D].rearrange("p (k n) -> p k n", n=D)
        meanw96 = src[0:DC, GROUP * D:GROUP * D + DC]
        turned, swapped = ([sb(f"{name}{i}", [PAIR, CROSS.project[0][1]]) for i in range(SLOTS)]
                           for name in ("turned", "swapped"))
        krot = sb("krot", [PAIR, CROSS.width])
        qrotb = [sb(f"qrot{i}", [PAIR, N]) for i in range(2)]
        K1b = [sb(f"K1_{i}", [D, 2, CROSS.width], F32R) for i in range(2)]
        K2b = [sb(f"K2_{i}", [STACK2, 2, CROSS.width], F32R) for i in range(2)]
        Q1b = [sb(f"Q1_{i}", [D, 2, 2, N], F32R) for i in range(2)]
        Q2b = [sb(f"Q2_{i}", [STACK2, 2, 2, N], F32R) for i in range(2)]
        Vb = [sb(f"V{i}", [D, len(CROSS.tiles), PAIR]) for i in range(2)]
        PR = [sb(f"P{i}", [D, 2, W]) for i in range(2)]
        psum_acc = sb("psum_acc", [D, 2, W])
        mx = sb("mx", [D, 4, len(CROSS.maxima)])
        nmx = sb("nmx", [D, 4])
        oraw = sb("oraw", [PAIR, N])
        oT = sb("oT", [PAIR, N])

        S = [ctx.enter_context(nc.psum_tensor(f"S{i}", [D, 2, W], F32)) for i in range(2)]
        PB = [ctx.enter_context(nc.psum_tensor(f"PB{i}", [D, 512], F32)) for i in range(BANKS)]
        OB = ctx.enter_context(nc.psum_tensor("OB", [D, 512], F32))

        def vpart(i, k):
            return Vb[i][:, 4 * k:4 * k + 4, :].rearrange("p a b -> p (a b)")

        xc = [PR[0][:, 0], PR[0][:, 1], PR[1][:, 0], PR[1][:, 1],
              psum_acc[:, 0], psum_acc[:, 1], krot[:, 0:512], krot[:, 512:1024]]
        sq, sd, rstd = [vpart(0, 0), vpart(0, 1)], vpart(1, 0), vpart(1, 1)
        w1_sb, w2_sb = vpart(0, 2), vpart(1, 2)
        hidden_sb = [psum_acc[:, 0], psum_acc[:, 1]]
        ada = vpart(0, 2)
        modt = vpart(1, 2)[:, 0:4 * B].rearrange("p (k b) -> p k b", b=B)

        s_const = sem("constants_loaded")
        s_ctx = sem("context_loaded")
        s_set = sem("constants_set")
        s_rows = sem("stack_rows_set")
        s_sel = sem("selectors_set")
        s_ada_mm = sem("adaln_products")
        s_mod = sem("adaln_vectors")
        s_bias = sem("biases_added")
        s_out = sem("output_stored")
        s_w1 = sem("ff_weights_loaded")
        s_h = sem("ff_hidden")
        s_g = sem("ff_gelu")
        s_f = sem("ff_out")
        s_y = sem("ff_added")

        class LayerNorm:

            def __init__(self, name):
                self.mean = sem(name + "_mean")
                self.centred = sem(name + "_centred")
                self.squared = sem(name + "_squared")
                self.var = sem(name + "_var")
                self.std = sem(name + "_std")
                self.inv = sem(name + "_inverse")
                self.cast = sem(name + "_broadcast")
                self.unit = sem(name + "_unit")
                self.done = sem(name + "_done")

        class Steps:

            def __init__(self, a):
                n = a.name
                self.src = sem(n + "_source_loaded")
                self.w = [sem(f"{n}_weights_loaded{i}") for i in range(2)]
                self.wo = [sem(f"{n}_wo_loaded{i}") for i in range(UNROLL)]
                self.proj = sem(n + "_projected")
                self.maxp = sem(n + "_max_scores")
                self.freed = sem(n + "_projection_turned")
                self.swap = [sem(f"{n}_swapped{i}") for i in range(SLOTS)]
                self.rot = sem(n + "_rotated")
                self.vread = sem(n + "_v_read")
                self.qh = sem(n + "_q_high")
                self.ql = sem(n + "_q_low")
                self.kh = sem(n + "_k_high")
                self.k2 = sem(n + "_k_high2")
                self.kl = sem(n + "_k_low")
                self.mxr = sem(n + "_max_reduced")
                self.mx = sem(n + "_max")
                self.mt = sem(n + "_max_row")
                self.mrow = sem(n + "_max_row_copied")
                self.s = sem(n + "_scores")
                self.e = sem(n + "_exp")
                self.pv = sem(n + "_pv")
                self.acc = sem(n + "_acc")
                self.fold = sem(n + "_fold")
                self.oev = sem(n + "_o_read")
                self.sum = sem(n + "_sum")
                self.inv = sem(n + "_sum_inverse")
                self.ot = sem(n + "_o_scaled")
                self.y = sem(n + "_y")
                self.added = sem(n + "_added")

        LN1, LNX, LN2, LN3 = LayerNorm("ln1"), LayerNorm("lnx"), LayerNorm("ln2"), LayerNorm("ln3")
        sems = {"sa": Steps(SELF), "ca": Steps(CROSS)}

        def run_steps(eng, a, body):
            for j in range(-a.lead, UNROLL):
                body((0, j))
            with eng.Fori(1, STEPS // UNROLL - 1) as i:
                for r in range(UNROLL):
                    body((i, r))
            for r in range(UNROLL + 1):
                body((STEPS // UNROLL - 1, r))

        def later(j, by):
            return (j[0], j[1] + by)

        def exists(j):
            return not isinstance(j[0], int) or 0 <= UNROLL * j[0] + j[1] < STEPS

        def times(j, n):
            return j[0] * (UNROLL * n) + j[1] * n

        def batch(j):
            return (j[0] + j[1] // UNROLL) >> 1

        def wait(eng, semaphore, value):
            if not isinstance(value, int) or value > 0:
                eng.wait_ge(semaphore, value)

        def of_step(a, what, j):
            by = 0 if what in ("S", "E", "P", "c", "oev") else -1 if what in ("sum", "div", "out", "add") else \
                1 if what in ("a", "mx", "M", "row") else a.lead
            return later(j, by)

        def slot(a, J):
            return J[1] % 2, J[1] % a.ring // 2

        def K1(a, J, rows, h, lo, hi):
            i, k = slot(a, J)
            return K1b[i][rows, h, k * N + lo:k * N + hi]

        def K2(a, J, rows, h, lo, hi):
            i, k = slot(a, J)
            return K2b[i][rows, h, k * N + lo:k * N + hi]

        def V(a, J, t):
            i, k = slot(a, J)
            return Vb[i][:, 2 * k + t, :]

        def Q1(a, J):
            i, k = slot(a, J)
            return Q1b[i][:, k]

        def Q2(a, J):
            i, k = slot(a, J)
            return Q2b[i][:, k]

        def half(h):
            return slice(h * DH, (h + 1) * DH)

        def context(c):
            return ctxT_all[:, bass.ds(c * CLN, CLN)]

        def slot_uses(a, J, m):
            return J[0] * (UNROLL * a.rotations // SLOTS) + (J[1] * a.rotations + m) // SLOTS

        def qrot(J):
            return qrotb[J[1] % 2]

        def krot_part(a, J, rows, k):
            lo, w = a.project[k]
            lo += J[1] % a.kept * N
            return krot[rows, lo:lo + w]

        def q_low(eng, a, s, J):
            wait(eng, s.qh, times(J, 1) + 1)
            for h in range(2):
                ins = eng.tensor_tensor(Q2(a, J)[0:DH, h, :], qrot(J)[half(h), :],
                                        Q1(a, J)[half(h), h, :].bitcast(F32), ALU.subtract)
            ins.then_inc(s.ql, 1)

        def k_low(eng, a, s, J, k):
            lo, w = a.project[k]
            wait(eng, s.kh, times(J, len(a.project)) + k + 1)
            for h in range(2):
                ins = eng.tensor_tensor(K1(a, J, half(1 - h), h, lo, lo + w),
                                        krot_part(a, J, half(h), k),
                                        K1(a, J, half(h), h, lo, lo + w).bitcast(F32), ALU.subtract)
            ins.then_inc(s.kl, 1)

        def run_groups(eng, count, order, run):
            words = [(w.rstrip("0123456789"), int("0" + w.lstrip("abcdefghijklmnopqrstuvwxyzABCDEFGHIJKLMNOPQRSTUVWXYZ")))
                     for w in order.split()]

            def body(g, r, new, old):
                for what, k in words:
                    if what.islower() and new:
                        run(what, g, k, r)
                    if what.isupper() and old:
                        run(what.lower(), g - 1, k, 1 - r)

            body(0, 0, True, False)
            if count > 2:
                body(1, 1, True, True)
                body(2, 0, True, True)
                with eng.Fori(1, count // 2 - 1) as i:
                    body(2 * i + 1, 1, True, True)
                    body(2 * i + 2, 0, True, True)
            if count > 1:
                body(count - 1, (count - 1) % 2, True, True)
            body(count, count % 2, False, True)

        block = ctx.enter_context(nc.Block())

        @block.sync
        def _(sp):
            for dst, source in ((cols, cols_in), (condT, cT_in), (ada, ada_in), (xT, xT_in),
                                (ropeq, rope_in[:, 2 * M:]), (ident, ident_in)):
                sp.dma_start(dst[:], source).then_inc(s_const, 16)

            def weights(a, s, J, pair):
                kv, wq, _ = packs[a.name]
                b = J[1] % 2
                n = len(a.count["proj"])
                wait(sp, s.proj, times(J, n) - n)
                sp.dma_start(kv_w[b][0:a.rows, :], kv[pair]).then_inc(s.w[b], 16)
                sp.dma_start(q_w[b][:, :], wq[pair]).then_inc(s.w[b], 16)

            def out_weights(a, s, J, pair):
                r = J[1] % UNROLL
                wait(sp, s.y, times(J, 1) - UNROLL + 1)
                sp.dma_start(o_w[r][:, :], packs[a.name][2][pair]).then_inc(s.wo[r], 16)

            def source(a, s, b):
                wait(sp, s.proj, b * (PAIRS * len(a.count["proj"])))
                keys = ainT if a is SELF else ctxT_all
                sp.dma_start(src[0:a.rows, 0:a.keys], keys[0:a.rows, bass.ds(b * a.keys, a.keys)]
                             ).then_inc(s.src, 16)

            def swap(a, s, J, m):
                i = (J[1] * a.rotations + m) % SLOTS
                w = N if m == 0 else a.project[m - 1][1]
                wait(sp, s.freed, times(J, a.rotations) + m + 1)
                for k in range(2):
                    sp.dma_start(swapped[i][k::2, 0:w], turned[i][1 - k::2, 0:w]).then_inc(s.swap[i], 16)

            def batch_of_steps(a, s, b, last):
                source(a, s, b)
                for r in range(PAIRS):
                    J, more = (b * 2, r), not (last and r == PAIRS - 1)
                    if more:
                        weights(a, s, later(J, 1), (r + 1) % PAIRS)
                    for m in range(a.rotations):
                        swap(a, s, J, m)
                    if more:
                        out_weights(a, s, later(J, 1), (r + 1) % PAIRS)
                    if a is SELF and isinstance(b, int) and b == 0:
                        sp.dma_start(ctxT_all[:, r * M:(r + 1) * M], ctxT_in[:, r * M:(r + 1) * M]
                                     ).then_inc(s_ctx, 16)

            for a, ln in ((SELF, LN1), (CROSS, LN2)):
                s = sems[a.name]
                if a is CROSS:
                    sp.wait_ge(sems["sa"].proj, len(SELF.count["proj"]) * STEPS)
                    sp.wait_ge(sems["sa"].y, STEPS)
                weights(a, s, (0, 0), 0)
                out_weights(a, s, (0, 0), 0)
                sp.wait_ge(ln.done, NLN)
                if a is CROSS:
                    sp.wait_ge(LNX.done, NCL)
                batch_of_steps(a, s, 0, False)
                if a is SELF:
                    sp.dma_start(cols96[:], cols96_in).then_inc(s_ctx, 16)
                    sp.dma_start(rope[:], rope_in[:, 0:2 * M]).then_inc(s_ctx, 16)
                with sp.Fori(1, B - 1) as b:
                    batch_of_steps(a, s, b, False)
                batch_of_steps(a, s, B - 1, True)
            s = sems["ca"]
            sp.wait_ge(s.pv, len(CROSS.chunks) * STEPS)
            sp.dma_start(w1_sb, w1_in).then_inc(s_w1, 16)
            sp.dma_start(w2_sb, w2_in).then_inc(s_w1, 16)
            for c in range(NLN):
                sp.wait_ge(s_y, c + 1)
                sp.dma_start(outT[:, c * LNC:(c + 1) * LNC], xT[:, c * LNC:(c + 1) * LNC]
                             ).then_inc(s_out, 16)
            sp.wait_ge(s_out, 16 * NLN)

        @block.gpsimd
        def _(pool):
            pool.memset(meanw[:], 1.0 / D).then_inc(s_set, 1)
            pool.memset(onesw[:], 1.0).then_inc(s_set, 1)
            pool.memset(epsc[:], EPS).then_inc(s_set, 1)
            pool.memset(ctxT_all[:, B * M:NCL * CLN], 0.0).then_inc(s_set, 1)

            def selectors(n):
                pool.memset(select[:], 0.0).then_inc(s_sel, 1)
                pool.memset(meanw96, 1.0 / DC).then_inc(s_sel, 1)
                pool.wait_ge(s_sel, (2 + GROUP) * (n - 1) + 2)
                for k in range(GROUP):
                    pool.memset(select[32 * k:32 * k + 1, k], 1.0).then_inc(s_sel, 1)
                    pool.wait_ge(s_sel, (2 + GROUP) * (n - 1) + k + 3)

            selectors(1)
            for i in range(2):
                pool.memset(K2b[i][DH:STACK2].bitcast(F32), 0.0).then_inc(s_rows, 1)
                pool.memset(Q2b[i][DH:STACK2].bitcast(F32), 0.0).then_inc(s_rows, 1)
            pool.wait_ge(s_rows, 4)
            for i in range(2):
                pool.memset(K2b[i][DH:DH + 1].bitcast(F32), 1.0).then_inc(s_rows, 1)
            pool.wait_ge(s_rows, 6)
            for i in range(2):
                pool.memset(K1b[i][:, :, CROSS.keys:CROSS.width].bitcast(F32), 0.0).then_inc(s_rows, 1)

            def attention(a, s):
                n, rows, last = len(a.chunks), a.tile, a.tiles[-1][1]

                def accumulate(j, c):
                    P = PR[(j[1] * n + c) % 2]
                    wait(pool, s.e, times(j, n) + c + 1)
                    if c == 1:
                        wait(pool, s.sum, times(j, 1))
                        pool.tensor_tensor(psum_acc[0:rows], PR[(j[1] * n) % 2][0:rows], P[0:rows], ALU.add
                                           ).then_inc(s.acc, 2)
                    elif c < n - 1:
                        wait(pool, s.acc, times(j, n) + c)
                        pool.tensor_tensor(psum_acc[0:rows], psum_acc[0:rows], P[0:rows], ALU.add
                                           ).then_inc(s.acc, 1)
                    else:
                        wait(pool, s.fold, times(j, 1) + 1)
                        pool.tensor_tensor(psum_acc[0:last, 0], psum_acc[0:last, 0], P[0:last, 0], ALU.add
                                           ).then_inc(s.acc, 1)
                    if c == n - 2:
                        wait(pool, s.acc, times(j, n) + c + 1)
                        pool.tensor_tensor(psum_acc[0:rows, 0], psum_acc[0:rows, 0], psum_acc[0:rows, 1],
                                           ALU.add).then_inc(s.fold, 1)

                def body(j):
                    for what, k in a.pool:
                        J = of_step(a, what, j)
                        if not exists(J):
                            continue
                        if what == "ql":
                            q_low(pool, a, s, J)
                        if what == "l":
                            k_low(pool, a, s, J, k)
                        if what == "c":
                            accumulate(J, k)

                run_steps(pool, a, body)

            attention(SELF, sems["sa"])
            pool.wait_ge(sems["sa"].kl, len(SELF.project) * STEPS)
            pool.wait_ge(sems["sa"].ql, STEPS)
            pool.wait_ge(sems["sa"].proj, len(SELF.count["proj"]) * STEPS)
            selectors(2)
            attention(CROSS, sems["ca"])
            pool.wait_ge(sems["ca"].proj, len(CROSS.count["proj"]) * STEPS)
            selectors(3)

        @block.scalar
        def _(act):
            def copy(out, in_):
                return act.activation(out, in_, ACT.Copy)

            def norm(ln, groups, rows, width, output):
                def square(c, k):
                    wait(act, ln.centred, c + 1)
                    wait(act, ln.var, c - 1)
                    act.activation(sq[k % 2][0:rows, 0:width], xc[k][0:rows, 0:width], ACT.Square
                                   ).then_inc(ln.squared, 1)

                def root(g, r):
                    wait(act, ln.var, (g + 1) * GROUP)
                    wait(act, ln.inv, g)
                    act.activation(sd[:, 0:width], (PB[2], OB)[r][:, 0:width], ACT.Sqrt, bias=epsc[:, :]
                                   ).then_inc(ln.std, 1)

                def affine(c, k):
                    wait(act, ln.unit, c + 1)
                    output(c, xc[k][0:rows, 0:width]).then_inc(ln.done, 1)

                def run(what, g, k, r):
                    if what == "square":
                        square(g * GROUP + k, r * GROUP + k)
                    if what == "root":
                        root(g, r)
                    if what == "out":
                        affine(g * GROUP + k, r * GROUP + k)

                run_groups(act, groups, "square0 square1 square2 OUT0 square3 OUT1 OUT2 OUT3 root", run)

            def adaln(ln, i):
                def output(c, unit):
                    for h in range(2):
                        b = 2 * c + h
                        ins = act.activation(ainT[:, b * N:(b + 1) * N], unit[:, h * N:(h + 1) * N],
                                             ACT.Identity, scale=mod[:, 2 * i, b:b + 1],
                                             bias=mod[:, 2 * i + 1, b:b + 1])
                    return ins

                norm(ln, NLN // GROUP, D, LNC, output)

            def context_out(c, unit):
                return act.activation(context(c), unit, ACT.Identity, scale=cols96[:, 0:1],
                                      bias=cols96[:, 1:2])

            def attention(a, s):
                n, nk, nv = len(a.chunks), len(a.project), len(a.vgroups)
                np_ = len(a.count["proj"])

                def exponentials(j, c):
                    rows, k, i = a.tiles[a.chunks[c][0]][1], len(a.chunks[c]), (j[1] * n + c) % 2
                    wait(act, s.s, times(j, n) + c + 1)
                    wait(act, s.pv, times(j, n) + c - 1)
                    if a is CROSS:
                        wait(act, s.acc, times(j, n) + c - 1)
                    else:
                        wait(act, s.sum, times(j, 1) - 1)
                    act.activation(PR[i][0:rows, 0:k], S[i][0:rows, 0:k], ACT.Exp, scale=SCALE
                                   ).then_inc(s.e, 1)

                def q_high(J):
                    wait(act, s.rot, times(J, 1 + nk) + 1)
                    wait(act, s.s, times(J, n) - n * (a.ring - 1))
                    for h in range(2):
                        for k in range(2):
                            ins = copy(Q1(a, J)[half(k), h, :], qrot(J)[half(h), :])
                    ins.then_inc(s.qh, 1)

                def k_high(J, k):
                    lo, w = a.project[k]
                    wait(act, s.rot, times(J, 1 + nk) + 2 + k)
                    wait(act, s.s, times(J, n) - n * (a.ring - 1))
                    for h in range(2):
                        ins = copy(K1(a, J, half(h), h, lo, lo + w), krot_part(a, J, half(h), k))
                    ins.then_inc(s.kh, 1)
                    for h in range(2):
                        ins = copy(K2(a, J, half(0), h, lo, lo + w), krot_part(a, J, half(h), k))
                    ins.then_inc(s.k2, 1)

                def v_out(J, v):
                    wait(act, s.proj, times(J, np_) + a.count["proj"].index(("v", v)) + 1)
                    wait(act, s.pv, times(J, n) - n * (a.ring - 1))
                    bank = PB[a.bank[("v", v)]]
                    ts = a.vgroups[v]
                    full = [t for t in ts if a.tiles[t][1] == a.tile]
                    i, k = slot(a, J)
                    if full:
                        ins = copy(Vb[i][0:a.tile, 2 * k + full[0]:2 * k + full[-1] + 1, :],
                                   bank[0:a.tile, 0:len(full) * PAIR].rearrange("p (t n) -> p t n", n=PAIR))
                    for t in ts:
                        if t not in full:
                            w = a.tiles[t][1]
                            at = (t - ts[0]) * PAIR
                            ins = copy(V(a, J, t)[0:w], bank[0:w, at:at + PAIR])
                    ins.then_inc(s.vread, 1)

                def max_row(J):
                    wait(act, s.mt, times(J, 1) + 1)
                    copy(Q2(a, J)[DH:DH + 1].rearrange("p h n -> p (h n)"), PB[a.bank[("M", 0)]][DH:DH + 1, :]
                         ).then_inc(s.mrow, 1)

                def o_out(j):
                    wait(act, s.pv, times(j, n) + n)
                    wait(act, s.ot, times(j, 1))
                    copy(oraw[:, :], OB[:, 0:N]).then_inc(s.oev, 1)

                def body(j):
                    for what, k in a.act:
                        J = of_step(a, what, j)
                        if not exists(J):
                            continue
                        if what == "E":
                            exponentials(J, k)
                        if what == "q":
                            q_high(J)
                        if what == "g":
                            k_high(J, k)
                        if what == "v":
                            v_out(J, k)
                        if what == "row":
                            max_row(J)
                        if what == "oev":
                            o_out(J)

                run_steps(act, a, body)

            act.wait_ge(s_set, 4)
            act.wait_ge(s_mod, 8)
            adaln(LN1, 0)
            act.wait_ge(s_rows, 8)
            attention(SELF, sems["sa"])
            adaln(LN2, 0)
            act.wait_ge(s_ctx, 16 * (B + 2))
            norm(LNX, NCL // GROUP, DC, CLN, context_out)
            attention(CROSS, sems["ca"])
            adaln(LN3, 1)
            for n in range(NLN * FF):
                f = n % FF
                act.wait_ge(s_h, n + 1)
                wait(act, s_f, n - 1)
                act.activation(hidden_sb[n % 2], PB[n % 2][:, :], ACT.Gelu, bias=cols[:, 12 + f:13 + f]
                               ).then_inc(s_g, 1)

        @block.vector
        def _(dve):
            def adaln_vectors():
                dve.wait_ge(s_ada_mm, 1)
                n = 0
                for i in range(2):
                    dve.tensor_scalar(modt[:, 2 * i, :], OB[:, 16 * i:16 * i + B], cols[:, 4 * i + 2:4 * i + 3],
                                      1.0, ALU.add, ALU.add).then_inc(s_mod, 1)
                    dve.tensor_scalar(modt[:, 2 * i + 1, :], OB[:, 16 * i + 8:16 * i + 8 + B],
                                      cols[:, 4 * i + 3:4 * i + 4], None, ALU.add).then_inc(s_mod, 1)
                    n += 2
                    dve.wait_ge(s_mod, n)
                    dve.tensor_scalar(mod[:, 2 * i, :], modt[:, 2 * i, :], cols[:, 4 * i:4 * i + 1], None,
                                      ALU.mult).then_inc(s_mod, 1)
                    dve.scalar_tensor_tensor(out=mod[:, 2 * i + 1, :], in0=modt[:, 2 * i, :],
                                             scalar=cols[:, 4 * i + 1:4 * i + 2], in1=modt[:, 2 * i + 1, :],
                                             op0=ALU.mult, op1=ALU.add).then_inc(s_mod, 1)
                    n += 2

            def norm(ln, groups, rows, width, x):
                def centre(c, k):
                    wait(dve, ln.mean, c + 1)
                    wait(dve, ln.done, c - 2 * GROUP + 1)
                    dve.tensor_tensor(xc[k][0:rows, 0:width], x(c), PB[k % 2][0:rows, 0:width], ALU.subtract
                                      ).then_inc(ln.centred, 1)

                def inverse(g):
                    wait(dve, ln.std, g + 1)
                    wait(dve, ln.cast, g * GROUP)
                    dve.reciprocal(rstd[:, 0:width], sd[:, 0:width]).then_inc(ln.inv, 1)

                def unit(c, k):
                    wait(dve, ln.cast, c + 1)
                    dve.tensor_tensor(xc[k][0:rows, 0:width], xc[k][0:rows, 0:width],
                                      S[k % GROUP // 2][0:rows, k % 2, 0:width], ALU.mult).then_inc(ln.unit, 1)

                def run(what, g, k, r):
                    if what == "centre":
                        centre(g * GROUP + k, r * GROUP + k)
                    if what == "inverse":
                        inverse(g)
                    if what == "unit":
                        unit(g * GROUP + k, r * GROUP + k)

                run_groups(dve, groups, "centre0 centre1 INVERSE centre2 UNIT0 centre3 UNIT1 UNIT2 UNIT3", run)

            def norm_x(ln):
                norm(ln, NLN // GROUP, D, LNC, lambda c: xT[:, c * LNC:(c + 1) * LNC])

            def add_bias(k, n):
                dve.tensor_scalar(xT[:, :], xT[:, :], cols[:, k:k + 1], None, ALU.add).then_inc(s_bias, 1)
                dve.wait_ge(s_bias, n)

            def attention(a, s):
                n, nk, nm = len(a.chunks), len(a.project), len(a.maxima)
                np_, na = len(a.count["proj"]), len(a.count["a"])
                table, per = (ropeq, N) if a is SELF else (rope, M)

                def multiply(J, w, m, cosines, sines, out, cols_):
                    i = (J[1] * a.rotations + m) % SLOTS
                    wait(dve, s.proj, times(J, np_) + a.count["proj"].index(w) + 1)
                    if m == 0:
                        wait(dve, s.qh, times(later(J, -1), 1))
                        wait(dve, s.ql, times(later(J, -1), 1))
                    if m == 1:
                        wait(dve, s.k2, times(later(J, 1 - a.kept), nk))
                        wait(dve, s.kl, times(later(J, 1 - a.kept), nk))
                    x = PB[a.bank[w]][:, 0:cols_]
                    dve.tensor_tensor(out, x, cosines, ALU.mult)
                    wait(dve, s.swap[i], slot_uses(a, J, m) * 32)
                    wait(dve, s.rot, times(J, 1 + nk) + m + 1 - SLOTS)
                    dve.tensor_tensor(turned[i][:, 0:cols_], x, sines, ALU.mult).then_inc(s.freed, 1)

                def add_swapped(J, m, out, cols_):
                    i = (J[1] * a.rotations + m) % SLOTS
                    wait(dve, s.swap[i], slot_uses(a, J, m) * 32 + 32)
                    dve.tensor_tensor(out, out, swapped[i][:, 0:cols_], ALU.add).then_inc(s.rot, 1)

                def maximum(J, k):
                    bank = PB[a.bank[("a", k)]]
                    wait(dve, s.maxp, times(J, na) + k + 1)
                    if a is SELF:
                        wait(dve, s.mt, times(J, 1))
                        dve.tensor_reduce(nmx[:, 2 * k:2 * k + 2], bank[:, :].rearrange("p (t n) -> p t n", n=N),
                                          AX.X, ALU.max, negate=True).then_inc(s.mxr, 1)
                    else:
                        c, hq = k // 4, k % 4
                        if k == 0:
                            wait(dve, s.mx, times(J, 1))
                        dve.tensor_reduce(mx[:, hq, c:c + 1], bank[:, 0:a.maxima[c][1]], AX.X, ALU.max
                                          ).then_inc(s.mxr, 1)

                def last_maximum(J):
                    wait(dve, s.mxr, times(J, na) + na)
                    wait(dve, s.mt, times(J, 1))
                    dve.tensor_reduce(nmx[:, :], mx[:, :, 0:nm], AX.X, ALU.max, negate=True
                                      ).then_inc(s.mx, 1)

                def divide(j):
                    wait(dve, s.sum, times(j, 1) + 1)
                    wait(dve, s.y, times(j, 1))
                    dve.reciprocal(oT[:, :], PB[a.bank[("sum", 0)]][:, 0:N]).then_inc(s.inv, 1)
                    wait(dve, s.inv, times(j, 1) + 1)
                    wait(dve, s.oev, times(j, 1) + 1)
                    dve.tensor_tensor(oT[:, :], oraw[:, :], oT[:, :], ALU.mult).then_inc(s.ot, 1)

                def add(j):
                    wait(dve, s.y, times(j, 1) + 1)
                    wait(dve, s.added, times(j, 1))
                    b = nc.s_assert_within(batch(j), 0, B - 1, skip_runtime_bounds_check_because=
                                           "there are PAIRS steps for each of the B batches")
                    dve.tensor_tensor(xT[:, bass.ds(b * N, N)], xT[:, bass.ds(b * N, N)],
                                      PB[a.bank[("out", 0)]][:, 0:N],
                                      ALU.add).then_inc(s.added, 1)

                def body(j):
                    for what, k in a.dve:
                        J = of_step(a, what, j)
                        if not exists(J):
                            continue
                        if what == "q":
                            multiply(J, (what, k), 0, ropeq[:, 0:N], ropeq[:, N:2 * N], qrot(J)[:, :], N)
                        if what == "k":
                            lo, w = a.project[k]
                            multiply(J, (what, k), 1 + k, table[:, lo:lo + w], table[:, per + lo:per + lo + w],
                                     krot_part(a, J, slice(0, D), k), w)
                        if what == "rq":
                            add_swapped(J, 0, qrot(J)[:, :], N)
                        if what == "r":
                            add_swapped(J, 1 + k, krot_part(a, J, slice(0, D), k), a.project[k][1])
                        if what == "ql":
                            q_low(dve, a, s, J)
                        if what == "l":
                            k_low(dve, a, s, J, k)
                        if what == "a":
                            maximum(J, k)
                        if what == "mx":
                            last_maximum(J)
                        if what == "div":
                            divide(J)
                        if what == "add":
                            add(J)

                run_steps(dve, a, body)
                dve.wait_ge(s.added, STEPS)

            dve.wait_ge(s_const, 16 * 6)
            adaln_vectors()
            norm_x(LN1)
            add_bias(8, 1)
            attention(SELF, sems["sa"])
            norm_x(LN2)
            add_bias(9, 2)
            dve.wait_ge(s_ctx, 16 * (B + 2))
            dve.wait_ge(LN2.done, NLN)
            norm(LNX, NCL // GROUP, DC, CLN, context)
            attention(CROSS, sems["ca"])
            norm_x(LN3)
            add_bias(10, 3)
            for c in range(NLN):
                dve.wait_ge(s_f, (c + 1) * FF)
                dve.tensor_tensor(xT[:, c * LNC:(c + 1) * LNC], xT[:, c * LNC:(c + 1) * LNC],
                                  (OB, PB[2])[c % 2][:, :], ALU.add).then_inc(s_y, 1)

        @block.tensor
        def _(pe):
            def norm(ln, groups, rows, width, x, weights):
                def mean(c, k):
                    wait(pe, ln.centred, c - 1)
                    pe.matmul(PB[k % 2][0:rows, 0:width], weights, x(c), start=True, stop=True
                              ).then_inc(ln.mean, 1)

                def variance(g, c, k, r):
                    wait(pe, ln.squared, c + 1)
                    if k == 0:
                        wait(pe, ln.std, g - 1)
                    pe.matmul((PB[2], OB)[r][32 * k:32 * k + 32, 0:width], weights[:, 0:32],
                              sq[k % 2][0:rows, 0:width], start=True, stop=True).then_inc(ln.var, 1)

                def spread(g, c, k):
                    wait(pe, ln.inv, g + 1)
                    wait(pe, ln.unit, c - GROUP + 1)
                    pe.matmul(S[k // 2][0:rows, k % 2, 0:width], select[:, k, 0:rows], rstd[:, 0:width],
                              start=True, stop=True).then_inc(ln.cast, 1)

                def run(what, g, k, r):
                    if what == "mean":
                        mean(g * GROUP + k, k)
                    if what == "var":
                        variance(g, g * GROUP + k, k, r)
                    if what == "spread":
                        spread(g, g * GROUP + k, k)

                run_groups(pe, groups, "mean0 mean1 var0 mean2 var1 mean3 SPREAD0 SPREAD1 var2 SPREAD2 var3 "
                           "SPREAD3", run)

            def norm_x(ln):
                norm(ln, NLN // GROUP, D, LNC, lambda c: xT[:, c * LNC:(c + 1) * LNC], meanw[:, :])

            def attention(a, s):
                n, nk, nv = len(a.chunks), len(a.project), len(a.vgroups)
                na = len(a.count["a"])

                def bank(J, w):
                    last, back = a.before[w]
                    k = later(J, -back)
                    while not exists(k) and isinstance(k[0], int) and k[1] > J[1] - 2 * UNROLL:
                        last, back = a.before[last]
                        k = later(k, -back)
                    if last[0] == "v":
                        wait(pe, s.vread, times(k, nv) + last[1] + 1)
                    elif last[0] == "a":
                        wait(pe, s.mxr, times(k, na) + last[1] + 1)
                    elif last[0] in ("M", "sum", "out"):
                        wait(pe, {"M": s.mrow, "sum": s.inv, "out": s.added}[last[0]], times(k, 1) + 1)
                    else:
                        wait(pe, s.freed, times(k, 1 + nk) + a.count["qk"].index(last) + 1)
                    return PB[a.bank[w]]

                def columns(J, keys, per, lo, w):
                    b = nc.s_assert_within(batch(J), 0, B - 1, skip_runtime_bounds_check_because=
                                           "there are PAIRS steps for each of the B batches")
                    return keys[:, bass.ds(b * per + lo, w)]

                def q_projection(J):
                    out = bank(J, ("q", 0))
                    b = J[1] % 2
                    wait(pe, s.w[b], (J[0] * 2 + J[1] // 2) * 32 + 32)
                    pe.matmul(out[:, 0:N], q_w[b][:, :], columns(J, ainT, N, 0, N), start=True, stop=True
                              ).then_inc(s.proj, 1)

                def k_projection(J, k):
                    out = bank(J, ("k", k))
                    b = J[1] % 2
                    lo, w = a.project[k]
                    pe.matmul(out[:, 0:w], kv_w[b][0:a.rows, 0:PAIR],
                              columns(J, ainT if a is SELF else ctxT_all, a.keys, lo, w),
                              start=True, stop=True).then_inc(s.proj, 1)

                def v_projection(J, v):
                    out = bank(J, ("v", v))
                    b = J[1] % 2
                    if v == 0:
                        wait(pe, s.w[b], (J[0] * 2 + J[1] // 2) * 32 + 32)
                        wait(pe, s.src, batch(J) * 16 + 16)
                    for k, t in enumerate(a.vgroups[v]):
                        lo, w = a.tiles[t]
                        ins = pe.matmul(out[0:w, k * PAIR:(k + 1) * PAIR], src[0:a.rows, lo:lo + w],
                                        kv_w[b][0:a.rows, PAIR:2 * PAIR], start=True, stop=True)
                    ins.then_inc(s.proj, 1)

                def max_scores(J, k):
                    out = bank(J, ("a", k))
                    if k == 0:
                        wait(pe, s.qh, times(J, 1) + 1)
                    if a is SELF:
                        wait(pe, s.kl, times(J, nk) + nk)
                        for qt in range(2):
                            ins = pe.matmul(out[:, qt * N:(qt + 1) * N], Q1(a, J)[:, k, qt * 128:(qt + 1) * 128],
                                            K1(a, J, slice(0, D), k, 0, N), start=True, stop=True)
                    else:
                        c, h, qt = k // 4, k % 4 // 2, k % 2
                        lo, w = a.maxima[c]
                        if h == qt == 0:
                            k = [i for i, (b, n_) in enumerate(a.project) if b + n_ >= lo + w][0]
                            wait(pe, s.kl, times(J, nk) + k + 1)
                        w += w % 2
                        ins = pe.matmul(out[:, 0:w], Q1(a, J)[:, h, qt * 128:(qt + 1) * 128],
                                        K1(a, J, slice(0, D), h, lo, lo + w), start=True, stop=True)
                    ins.then_inc(s.maxp, 1)

                def max_row(J):
                    out = bank(J, ("M", 0))
                    if a is SELF:
                        wait(pe, s.mxr, times(J, na) + na)
                    else:
                        wait(pe, s.mx, times(J, 1) + 1)
                    for hq in range(4):
                        ins = pe.matmul(out[DH:DH + 1, hq * 128:(hq + 1) * 128], nmx[:, hq:hq + 1],
                                        ident[:, :], start=True, stop=True)
                    ins.then_inc(s.mt, 1)

                def scores(j, c):
                    i = (j[1] * n + c) % 2
                    if c == 0:
                        wait(pe, s.k2, times(j, nk) + nk)
                        wait(pe, s.kl, times(j, nk) + nk)
                        wait(pe, s.ql, times(j, 1) + 1)
                        wait(pe, s.mrow, times(j, 1) + 1)
                    wait(pe, s.e, times(j, n) + c - 1)
                    for k, t in enumerate(a.chunks[c]):
                        lo, w = a.tiles[t]
                        for h in range(2):
                            out = S[i][0:w, k, h * N:(h + 1) * N]
                            pe.matmul(out, K1(a, j, slice(0, D), h, lo, lo + w), Q1(a, j)[:, h, :],
                                      start=True, stop=False)
                            ins = pe.matmul(out, K2(a, j, slice(0, STACK2), h, lo, lo + w), Q2(a, j)[:, h, :],
                                            start=False, stop=True)
                    ins.then_inc(s.s, 1)

                def products(j, c):
                    i = (j[1] * n + c) % 2
                    if c == 0:
                        wait(pe, s.vread, times(j, nv) + nv)
                        wait(pe, s.oev, times(j, 1))
                    wait(pe, s.e, times(j, n) + c + 1)
                    for k, t in enumerate(a.chunks[c]):
                        w = a.tiles[t][1]
                        for h in range(2):
                            ins = pe.matmul(OB[half(h), 0:N], V(a, j, t)[0:w, half(h)],
                                            PR[i][0:w, k, h * N:(h + 1) * N], start=(t == 0),
                                            stop=(t == len(a.tiles) - 1))
                    ins.then_inc(s.pv, 1)

                def sums(j):
                    out = bank(j, ("sum", 0))
                    if a is SELF:
                        parts = (PR[j[1] % 2][:, 0], PR[j[1] % 2][:, 1])
                    else:
                        wait(pe, s.acc, times(j, n) + n)
                        parts = (psum_acc[0:a.tile, 0],)
                    for h in range(2):
                        for k, p in enumerate(parts):
                            ins = pe.matmul(out[half(h), 0:N], onesw[0:a.tile, :], p[:, h * N:(h + 1) * N],
                                            start=(k == 0), stop=(k == len(parts) - 1))
                    ins.then_inc(s.sum, 1)

                def output(j):
                    r = j[1] % UNROLL
                    wait(pe, s.wo[r], (j[0] + j[1] // UNROLL) * 16 + 16)
                    wait(pe, s.ot, times(j, 1) + 1)
                    out = bank(j, ("out", 0))
                    pe.matmul(out[:, 0:N], o_w[r][:, :], oT[:, :], start=True, stop=True).then_inc(s.y, 1)

                def body(j):
                    for what, k in a.pe:
                        J = of_step(a, what, j)
                        if not exists(J):
                            continue
                        if what == "S":
                            scores(J, k)
                        if what == "P":
                            products(J, k)
                        if what == "q":
                            q_projection(J)
                        if what == "k":
                            k_projection(J, k)
                        if what == "v":
                            v_projection(J, k)
                        if what == "a":
                            max_scores(J, k)
                        if what == "M":
                            max_row(J)
                        if what == "sum":
                            sums(J)
                        if what == "out":
                            output(J)

                run_steps(pe, a, body)
                pe.wait_ge(s.added, STEPS)

            pe.wait_ge(s_const, 16 * 6)
            pe.wait_ge(s_set, 4)
            pe.wait_ge(s_sel, 2 + GROUP)
            for i in range(4):
                ins = pe.matmul(OB[:, 8 * i:8 * i + B], ada[:, i * D:(i + 1) * D], condT[:, :], start=True,
                                stop=True)
            ins.then_inc(s_ada_mm, 1)
            norm_x(LN1)
            pe.wait_ge(LN1.done, NLN)
            pe.wait_ge(s_rows, 8)
            attention(SELF, sems["sa"])
            pe.wait_ge(s_sel, 2 * (2 + GROUP))
            norm_x(LN2)
            pe.wait_ge(s_ctx, 16 * (B + 2))
            norm(LNX, NCL // GROUP, DC, CLN, context, meanw96[:, :])
            pe.wait_ge(LN2.done, NLN)
            pe.wait_ge(LNX.done, NCL)
            attention(CROSS, sems["ca"])
            pe.wait_ge(s_sel, 3 * (2 + GROUP))
            norm_x(LN3)
            pe.wait_ge(s_w1, 32)

            def hidden(n):
                c, f = n // FF, n % FF
                pe.wait_ge(LN3.done, c + 1)
                wait(pe, s_g, n - 1)
                pe.matmul(PB[n % 2][:, :], w1_sb[:, f * D:(f + 1) * D], ainT[:, c * LNC:(c + 1) * LNC],
                          start=True, stop=True).then_inc(s_h, 1)

            hidden(0)
            for n in range(NLN * FF):
                c, f = n // FF, n % FF
                if n + 1 < NLN * FF:
                    hidden(n + 1)
                pe.wait_ge(s_g, n + 1)
                if f == 0:
                    wait(pe, s_y, c - 1)
                pe.matmul((OB, PB[2])[c % 2][:, :], w2_sb[:, f * D:(f + 1) * D], hidden_sb[n % 2],
                          start=(f == 0), stop=(f == FF - 1)).then_inc(s_f, 1)


def kernel(**inputs):
    import concourse.bacc as bacc
    from concourse.bass_utils import run_bass_kernel_spmd

    a = {k.removeprefix("L0_xcond_"): np.asarray(v) for k, v in inputs.items()}
    B, n, D_ = a["x"].shape
    M = a["ctx_768"].shape[1]
    pairs = a["sa_wq"].shape[1] // PAIR

    def by_pair(w):
        return w.reshape(w.shape[0], pairs, PAIR).transpose(1, 0, 2)

    def packs(p):
        wk, wv = np.split(a[p + "_wkv"], 2, axis=1)
        return np.concatenate([by_pair(wk), by_pair(wv)], axis=2), by_pair(a[p + "_wq"]), \
            a[p + "_wo"].reshape(pairs, PAIR, D_)

    inv = np.float32(1) / (10000.0 ** (np.arange(0, DH, 2) / DH)).astype(np.float32)
    ang = np.arange(M, dtype=np.float32)[:, None] * inv[None, :]
    cos, sin = np.cos(ang).T, np.sin(ang).T
    C = np.tile(np.repeat(cos, 2, axis=0), (2, 1))
    Sg = np.tile(np.stack([sin, -sin], axis=1).reshape(DH, M), (2, 1))
    rope = np.concatenate([C, Sg, C[:, :n], Sg[:, :n]], axis=1)
    ff = a["ff_w1"].shape[1] // D_
    cols = np.stack([a["ln1_w"], a["ln1_b"], a["g1_b"], a["b1_b"], a["ln2_w"], a["ln2_b"], a["g2_b"],
                     a["b2_b"], a["sa_bo"], a["ca_bo"], a["ff_b2"], a["ff_b2"]]
                    + list(a["ff_b1"].reshape(ff, D_)), axis=1)
    arrays = {
        "xT": a["x"].transpose(2, 0, 1).reshape(D_, B * n),
        "condT": a["cond_1024"].T,
        "ctxT": a["ctx_768"].transpose(2, 0, 1).reshape(-1, B * M),
        "cols": cols,
        "cols96": np.stack([a["ca_lnc_w"], a["ca_lnc_b"]], axis=1),
        "ada": np.concatenate([a["g1_w"], a["b1_w"], a["g2_w"], a["b2_w"]], axis=1),
        "w1": a["ff_w1"],
        "w2": a["ff_w2"].reshape(ff, D_, D_).transpose(1, 0, 2).reshape(D_, ff * D_),
        "rope": rope,
        "ident": np.eye(D_, dtype=np.float32),
    }
    for p in ("sa", "ca"):
        for name, w in zip(("kv", "wq", "wo"), packs(p)):
            arrays[f"{p}_{name}"] = w
    arrays = {k: np.ascontiguousarray(v) for k, v in arrays.items()}

    nc = bacc.Bacc("TRN2", target_bir_lowering=False, num_devices=1)
    t = {k: nc.dram_tensor(k + "_dram", v.shape, F32, kind="ExternalInput").ap() for k, v in arrays.items()}
    out = nc.dram_tensor("outT_dram", (D_, B * n), F32, kind="ExternalOutput").ap()
    block_kernel(nc, t["xT"], t["condT"], t["ctxT"], t["cols"], t["cols96"], t["ada"],
                 {p: (t[p + "_kv"], t[p + "_wq"], t[p + "_wo"]) for p in ("sa", "ca")},
                 t["w1"], t["w2"], t["rope"], t["ident"], out)
    r = run_bass_kernel_spmd(nc, [{k + "_dram": v for k, v in arrays.items()}], core_ids=[0])
    return r.results[0]["outT_dram"].reshape(D_, B, n).transpose(1, 2, 0)
```
